# Optimizing a Trainium2 kernel written in Bass

```python
import numpy as np
import jax
import jax.numpy as jnp

def _softmax(x, axis=-1):
    return jax.nn.softmax(x, axis=axis)

def _gelu(x):
    return jax.nn.gelu(x, approximate=True)

def _silu(x):
    return jax.nn.silu(x)

def _sigmoid(x):
    return jax.nn.sigmoid(x)

def _layernorm(x, axis=-1, eps=1e-05):
    m = jnp.mean(x, axis=axis, keepdims=True)
    v = jnp.var(x, axis=axis, keepdims=True)
    return (x - m) / jnp.sqrt(v + eps)

def _scatter_add(tgt, idx, src, axis=0):
    return tgt.at[idx].add(src)

def _segment_sum(src, seg, n):
    return jax.ops.segment_sum(src, seg, n)
kernel_name = 'mk_xattn_ffn_d1_seqx_r8_073fe8'

def setup_inputs(seed: int=0):
    np.random.seed(seed)
    _w = jnp.asarray

    def _rec_inputs():
        import jax
        import jax.numpy as jnp
        _rk = jax.random.key(seed)
        x = 7.22e-05 + 1 * jax.random.normal(jax.random.fold_in(_rk, 1), (8, 128, 256), jnp.float32)
        _lenS = 128 - jax.random.randint(jax.random.fold_in(_rk, 7), (8,), 0, max(1, 128 // 4) + 1, jnp.int32)
        _lenS2 = 128 - jax.random.randint(jax.random.fold_in(_rk, 8), (8,), 0, max(1, 128 // 4) + 1, jnp.int32)
        _ctx_512P = jax.random.normal(jax.random.fold_in(_rk, 11), (8, 16, 64), jnp.float32)
        _ctx_512c = jax.random.dirichlet(jax.random.fold_in(_rk, 511), 0.3 * jnp.ones((16,), jnp.float32), (8, 128))
        _ctx_512t = jnp.einsum('bsk,bkd->bsd', _ctx_512c, _ctx_512P)
        _ctx_512t = _ctx_512t * jax.lax.rsqrt(jnp.mean(jnp.square(_ctx_512t)) + 1e-12) * 0.953939
        ctx_512 = -0.000514642 + 1.00011 * (_ctx_512t + 0.3 * jax.random.normal(jax.random.fold_in(_rk, 611), (8, 128, 64), jnp.float32))
        return (x, ctx_512)
    x, ctx_512 = _rec_inputs()

    def _L0_xattn_setup():
        import jax, jax.numpy as jnp
        import numpy as np
        B, S, H, NH, L = (2, 256, 256, 16, 64)
        HD = H // NH
        key = jax.random.key(seed)
        k1, k2, k3, k4, k5 = jax.random.split(key, 5)
        scale = 0.02
        return {'q': jax.random.normal(k1, (B, S, H), dtype=jnp.float32), 'latent_kv': jax.random.normal(k2, (B, S, L), dtype=jnp.float32), 'Wq': jax.random.normal(k3, (H, H), dtype=jnp.float32) * scale, 'Wkv_expand': jax.random.normal(k4, (2 * H, L), dtype=jnp.float32) * scale, 'Wout': jax.random.normal(k5, (H, H), dtype=jnp.float32) * scale}
    _L0_xattn_all = _L0_xattn_setup()
    _L0_xattn_in = {k: v for k, v in _L0_xattn_all.items() if k in ('Wq', 'Wkv_expand', 'Wout')}
    del _L0_xattn_all

    def _L0_ffn_setup():
        import jax, jax.numpy as jnp
        import numpy as np
        TOP_K = 2
        SCALING = 2.0
        key = jax.random.key(seed)
        ks = jax.random.split(key, 10)
        B, S, H, I, E, R = (1, 64, 256, 128, 8, 16)
        w = 1.0 / np.sqrt(H)
        inp = {'x': jax.random.normal(ks[0], (B, S, H), jnp.float32), 'gate_weight': jax.random.normal(ks[1], (E, H), jnp.float32) * w, 'gate_lora_A': jax.random.normal(ks[2], (R, H), jnp.float32) * 0.02, 'gate_lora_B': jax.random.normal(ks[3], (E, R), jnp.float32) * 0.02, 'gate_up_proj': jax.random.normal(ks[4], (E, H, 2 * I), jnp.float32) * w, 'down_proj': jax.random.normal(ks[5], (E, I, H), jnp.float32) * (1.0 / np.sqrt(I)), 'gup_lora_A': jax.random.normal(ks[6], (E, R, H), jnp.float32) * 0.02, 'gup_lora_B': jax.random.normal(ks[7], (E, 2 * I, R), jnp.float32) * 0.02, 'down_lora_A': jax.random.normal(ks[8], (E, R, I), jnp.float32) * 0.02, 'down_lora_B': jax.random.normal(ks[9], (E, H, R), jnp.float32) * 0.02}
        return inp
    _L0_ffn_all = _L0_ffn_setup()
    _L0_ffn_in = {k: v for k, v in _L0_ffn_all.items() if k in ('gate_weight', 'gate_lora_A', 'gate_lora_B', 'gate_up_proj', 'down_proj', 'gup_lora_A', 'gup_lora_B', 'down_lora_A', 'down_lora_B')}
    del _L0_ffn_all
    return {'x': x, 'ctx_512': ctx_512, 'L0_xattn_Wq': _L0_xattn_in['Wq'], 'L0_xattn_Wkv_expand': _L0_xattn_in['Wkv_expand'], 'L0_xattn_Wout': _L0_xattn_in['Wout'], 'L0_ffn_gate_weight': _L0_ffn_in['gate_weight'], 'L0_ffn_gate_lora_A': _L0_ffn_in['gate_lora_A'], 'L0_ffn_gate_lora_B': _L0_ffn_in['gate_lora_B'], 'L0_ffn_gate_up_proj': _L0_ffn_in['gate_up_proj'], 'L0_ffn_down_proj': _L0_ffn_in['down_proj'], 'L0_ffn_gup_lora_A': _L0_ffn_in['gup_lora_A'], 'L0_ffn_gup_lora_B': _L0_ffn_in['gup_lora_B'], 'L0_ffn_down_lora_A': _L0_ffn_in['down_lora_A'], 'L0_ffn_down_lora_B': _L0_ffn_in['down_lora_B']}

def reference(x, ctx_512, L0_xattn_Wq, L0_xattn_Wkv_expand, L0_xattn_Wout, L0_ffn_gate_weight, L0_ffn_gate_lora_A, L0_ffn_gate_lora_B, L0_ffn_gate_up_proj, L0_ffn_down_proj, L0_ffn_gup_lora_A, L0_ffn_gup_lora_B, L0_ffn_down_lora_A, L0_ffn_down_lora_B):
    import jax
    import jax.numpy as jnp

    def _L0_xattn_ref(q, latent_kv, Wq, Wkv_expand, Wout):
        import jax, jax.numpy as jnp
        import numpy as np
        B, S, H, NH, L = (2, 256, 256, 16, 64)
        HD = H // NH
        b, sq, _ = q.shape
        sk = latent_kv.shape[1]
        qp = q @ Wq.T
        kv = latent_kv @ Wkv_expand.T
        k, v = jnp.split(kv, 2, axis=-1)
        qh = qp.reshape(b, sq, NH, HD).transpose(0, 2, 1, 3)
        kh = k.reshape(b, sk, NH, HD).transpose(0, 2, 1, 3)
        vh = v.reshape(b, sk, NH, HD).transpose(0, 2, 1, 3)
        inv_sqrt_d = 1.0 / jnp.sqrt(jnp.float32(HD))
        scores = jnp.einsum('bhqd,bhkd->bhqk', qh, kh) * inv_sqrt_d
        causal = jnp.tril(jnp.ones((sq, sk), dtype=bool))
        scores = jnp.where(causal, scores, jnp.finfo(scores.dtype).min)
        attn = jax.nn.softmax(scores, axis=-1)
        out = jnp.einsum('bhqk,bhkd->bhqd', attn, vh)
        out = out.transpose(0, 2, 1, 3).reshape(b, sq, H)
        return out @ Wout.T

    def _L0_ffn_ref(x, gate_weight, gate_lora_A, gate_lora_B, gate_up_proj, down_proj, gup_lora_A, gup_lora_B, down_lora_A, down_lora_B):
        import jax, jax.numpy as jnp
        import numpy as np
        TOP_K = 2
        SCALING = 2.0
        B, S, H = x.shape
        xf = x.reshape(-1, H)
        gate_delta = SCALING * (gate_lora_B @ gate_lora_A)
        router_logits = xf @ gate_weight.T + xf @ gate_delta.T
        probs = jax.nn.softmax(router_logits.astype(jnp.float32), axis=-1)
        routing_weights, selected = jax.lax.top_k(probs, TOP_K)
        routing_weights = routing_weights / routing_weights.sum(-1, keepdims=True)
        routing_weights = routing_weights.astype(xf.dtype)
        gup = jnp.einsum('th,eho->teo', xf, gate_up_proj)
        gup = gup + SCALING * jnp.einsum('ter,eor->teo', jnp.einsum('th,erh->ter', xf, gup_lora_A), gup_lora_B)
        gates, h = jnp.split(gup, 2, axis=-1)
        h = jax.nn.silu(gates) * h
        out = jnp.einsum('tei,eih->teh', h, down_proj)
        out = out + SCALING * jnp.einsum('ter,ehr->teh', jnp.einsum('tei,eri->ter', h, down_lora_A), down_lora_B)
        out_sel = jnp.take_along_axis(out, selected[:, :, None], axis=1)
        y = jnp.einsum('tkh,tk->th', out_sel, routing_weights)
        return y.reshape(B, S, H)
    x = x + _L0_xattn_ref(_layernorm(x, axis=-1), ctx_512, L0_xattn_Wq, L0_xattn_Wkv_expand, L0_xattn_Wout)
    x = x + _L0_ffn_ref(_layernorm(x, axis=-1), L0_ffn_gate_weight, L0_ffn_gate_lora_A, L0_ffn_gate_lora_B, L0_ffn_gate_up_proj, L0_ffn_down_proj, L0_ffn_gup_lora_A, L0_ffn_gup_lora_B, L0_ffn_down_lora_A, L0_ffn_down_lora_B)
    return x

_drawn_inputs = setup_inputs


def setup_inputs(seed=0):
    import zlib

    import numpy as np

    out = dict(_drawn_inputs(seed))
    spreads = {}
    factors = {'L0_xattn_Wq': 24.096, 'L0_ffn_down_lora_A': 3.872, 'L0_ffn_down_lora_B': 3.886}
    for name, (base, spread) in spreads.items():
        noise = np.random.default_rng([zlib.crc32(name.encode()), seed]).standard_normal(out[name].shape)
        drawn = base * np.exp(spread * noise) if base else spread * noise
        out[name] = jnp.asarray(drawn.astype(out[name].dtype))
    for name, factor in factors.items():
        out[name] = (out[name] * factor).astype(out[name].dtype)
    return out
```

```python
import concourse.bass as bass
from concourse import mybir
from contextlib import ExitStack

F32 = mybir.dt.float32
F32R = mybir.dt.float32r
BF16 = mybir.dt.bfloat16
ALU = mybir.AluOpType
ACT = mybir.ActivationFunctionType
AX = mybir.AxisListType


def cross_attention_moe_kernel(nc, x, ctx_kv, Wq, Wkv, Wout, gate_w, gate_A, gate_B,
                               gate_up, down, gup_A, gup_B, down_A, down_B, out):
    P = 128
    B, S, H = x.shape
    L = ctx_kv.shape[2]
    HD = 16
    NH = H // HD
    E = gate_w.shape[0]
    R = gate_A.shape[0]
    I = down.shape[1]
    HC = H // P
    NT = B
    GT = 4
    NG = NT // GT
    GN = GT * P
    NC = NH // 4
    VW = HD + 1
    SLOTS_Q = (0, 0, 1, 1, 0, 2)
    SLOTS_K = (0, 1, 0, 1, 2, 0)
    NS = len(SLOTS_Q)
    KS = NS * HD
    KM = KS + 3
    SCALE = 0.25
    LORA = 2.0
    EPS = 1e-5
    MASKED = -2.0 ** 127
    ORDER = (2, 3, 0, 1)
    ROUTER_AT = (GT + 1,)
    LORA_BANK = lambda n: (5, 6, 7)[n % 3]

    ctx = ExitStack()
    with ctx:
        def sb(name, shape, dt=F32):
            return ctx.enter_context(nc.sbuf_tensor(name, shape, dt))

        def sem(name):
            return ctx.enter_context(nc.semaphore(name))

        x_sb = sb("x_sb", [P, NT, H])
        ctx_sb = sb("ctx_sb", [P, NT, 2, L])
        wq_raw = sb("wq_raw", [P, HC, H])
        wkv_raw = sb("wkv_raw", [P, 2 * HC, 2, L])
        wo_raw = sb("wo_raw", [P, HC, H])
        gw_raw = sb("gw_raw", [E, H])
        ga_raw = sb("ga_raw", [R, H])
        gb_raw = sb("gb_raw", [E, R])
        gbT = sb("gbT", [R, E])
        wqT_hi = sb("wqT_hi", [P, HC, H], F32R)
        wqT_lo = sb("wqT_lo", [P, HC, H], F32R)
        wkv_hi = sb("wkv_hi", [P, 2 * H], F32R)
        wkv_lo = sb("wkv_lo", [P, 2 * H], F32R)
        woT_hi = sb("woT_hi", [P, HC, H], F32R)
        woT_lo = sb("woT_lo", [P, HC, H], F32R)
        wr_hi = sb("wr_hi", [P, HC, P], F32R)
        wr_lo = sb("wr_lo", [P, HC, P], F32R)
        upA_raw = sb("upA_raw", [P, H])
        upB_raw = sb("upB_raw", [P, HC, E, R])
        dnA_raw = sb("dnA_raw", [P, I])
        dnB_raw = sb("dnB_raw", [P, HC, E, R])
        loraBT = sb("loraBT", [P, 2, H])
        expert_rows = sb("expert_rows", [P, E])
        up_w = sb("up_w", [P, HC, E, 2 * I])
        dn_w = sb("dn_w", [P, E, H])
        ffn_buf = up_w[:, :, :, :].rearrange("p a e n -> p (a e n)")
        silu = ffn_buf[:, 0:2 * GN].rearrange("p (k n) -> p k n", k=2)
        gated = ffn_buf[:, 2 * GN:4 * GN].rearrange("p (k n) -> p k n", k=2)
        h_f = ffn_buf[:, 4 * GN:6 * GN].rearrange("p (k n) -> p k n", k=2)
        up_hi = sb("up_hi", [P, HC, E, 2 * I], F32R)
        dn_hi = sb("dn_hi", [P, E, H], F32R)
        arena = sb("arena", [P, 2, NH, P])
        upA_bd = arena[:, 0, :, :].rearrange("p h n -> p (h n)").rearrange("p (e n) -> p e n", e=E)
        dnA_bd = arena[:, 1, 0:E, :]
        probsT = arena
        q_st = sb("q_st", [KM, 3, NH, P], BF16)
        k_st = sb("k_st", [KM, 3, NH, P], BF16)
        v_sb = sb("v_sb", [P, NT, NH, VW])
        xT_hi = sb("xT_hi", [P, HC, NT * P], F32R)
        xT_lo = sb("xT_lo", [P, HC, NT * P], F32R)
        ident = sb("ident", [P, P])
        ident_b = sb("ident_b", [P, P], BF16)
        causal = sb("causal", [P, 4, P], BF16)
        stats = sb("stats", [P, 2, NT, 6])
        mv = sb("mv", [P, 2, NT, 2])
        rstd = sb("rstd", [P, 2, NT])
        var_eps = sb("var_eps", [P, NT])
        minus_half = sb("minus_half", [P, NT])
        m_sb = sb("m_sb", [P, 2, NH])
        m_rest = sb("m_rest", [P, NH])
        m_parts = sb("m_parts", [P, 3, NH], BF16)
        mT = sb("mT", [3 * NH, P], BF16)
        oT_sb = sb("oT_sb", [P, 4, P])
        r_den = sb("r_den", [P, 4, 4])
        o_nat = sb("o_nat", [P, NH, HD])
        oT_hi = sb("oT_hi", [P, HC, P], F32R)
        oT_lo = sb("oT_lo", [P, HC, P], F32R)
        x2hat = sb("x2hat", [P, H])
        lgT = sb("lgT", [E, GN])
        lg = sb("lg", [P, GT, E])
        lmax = sb("lmax", [P, GT])
        above = sb("above", [P, GT, E, E])
        equal = sb("equal", [P, GT, E, E])
        earlier = sb("earlier", [P, E, E])
        rank = sb("rank", [P, GT, E])
        chosen = sb("chosen", [P, GT, E])
        lsub = sb("lsub", [P, GT, E])
        lexp = sb("lexp", [P, GT, E])
        lpick = sb("lpick", [P, GT, E])
        lsum = sb("lsum", [P, GT])
        linv = sb("linv", [P, GT])
        wts = sb("wts", [P, GT, E])
        w_rest = sb("w_rest", [P, GT, E])
        w_parts = sb("w_parts", [P, GT, 3, E], BF16)
        wT = sb("wT", [3 * E, NG, GN], BF16)
        pick = sb("pick", [3 * E, E, P], BF16)
        h_hi = sb("h_hi", [P, 2, GN], F32R)
        h_lo = sb("h_lo", [P, 2, GN], F32R)

        with ExitStack() as early:
            def sbe(name, shape, dt=F32):
                return early.enter_context(nc.sbuf_tensor(name, shape, dt))
            parts = sbe("parts", [P, 4, 3, GN], BF16)
            rest = sbe("rest", [P, 2, GN])
            xhat = sbe("xhat", [P, GT, H])
            cT = sbe("cT", [P, GN], F32R)
            cT_tmp = sbe("cT_tmp", [P, GN], F32R)
        up_lo = sb("up_lo", [P, HC, E, 2 * I], F32R)
        dn_lo = sb("dn_lo", [P, E, H], F32R)

        qk_dram = nc.dram_tensor("qk_parts", (2, NT, HC, 3, HD, NH // HC, P), BF16, kind="Internal").ap()

        bank = [ctx.enter_context(nc.psum_tensor(f"bank{i}", [P, 512], F32)) for i in range(8)]

        QK_BANK = lambda j: bank[(5, 6, 7, 2)[j]]

        ld = {n: sem("ld_" + n) for n in ("x0", "x1", "ctx", "wq", "wkv", "wo", "gate", "upA", "upB",
                                          "dnA", "dnB", "up", "dn")}
        stack_loaded = [sem(f"stack_loaded{i}") for i in range(3)]
        m_loaded = [sem(f"m_loaded{i}") for i in range(2)]
        made = {}

        def S_(name):
            if name not in made:
                made[name] = sem(name)
            return made[name]

        lgT_rows = lgT
        xT_src = lambda g: slice(g * GN, (g + 1) * GN)
        ctx_v = ctx_kv.rearrange("b s l -> s b l")
        x_v = x.rearrange("b s h -> s b h")
        out_v = out.rearrange("b s h -> s b h")
        wkv_v = Wkv.rearrange("(c p) l -> p c l", p=P)

        block = ctx.enter_context(nc.Block())

        @block.sync
        def _(sp):
            for g in range(NG):
                if g == 0:
                    sp.dma_start(x_sb[:, 0:GT, :], x_v[:, 0:GT, :]).then_inc(ld["x0"], 16)
                    for k in range(2):
                        sp.dma_start(wkv_raw[:, :, k, :], wkv_v).then_inc(ld["wkv"], 16)
                    for k in range(2):
                        sp.dma_start(ctx_sb[:, :, k, :], ctx_v).then_inc(ld["ctx"], 16)
                    sp.dma_start(wq_raw[:, :, :], Wq.rearrange("(c p) h -> p c h", p=P)).then_inc(ld["wq"], 16)
                else:
                    sp.dma_start(x_sb[:, GT:NT, :], x_v[:, GT:NT, :]).then_inc(ld["x1"], 16)
            sp.dma_start(upA_raw[:, :], gup_A.rearrange("e r h -> (e r) h")).then_inc(ld["upA"], 16)
            sp.dma_start(dnA_raw[:, :], down_A.rearrange("e r i -> (e r) i")).then_inc(ld["dnA"], 16)
            for c in range(HC):
                sp.dma_start(upB_raw[:, c, :, :], gup_B.rearrange("e (c p) r -> c p e r", p=P)[c]).then_inc(ld["upB"], 16)
            for c in range(HC):
                sp.dma_start(dnB_raw[:, c, :, :], down_B.rearrange("e (c p) r -> c p e r", p=P)[c]).then_inc(ld["dnB"], 16)
            sp.dma_start(wo_raw[:, :, :], Wout.rearrange("(c p) h -> p c h", p=P)).then_inc(ld["wo"], 16)
            sp.dma_start(gw_raw[:, :], gate_w).then_inc(ld["gate"], 16)
            sp.dma_start(ga_raw[:, :], gate_A).then_inc(ld["gate"], 16)
            sp.dma_start(gb_raw[:, :], gate_B).then_inc(ld["gate"], 16)
            for c in range(HC):
                sp.dma_start(up_w[:, c, :, :], gate_up.rearrange("e (c p) o -> c p e o", p=P)[c]).then_inc(ld["up"], 16)
            sp.dma_start(dn_w[:, :, :], down.rearrange("e i h -> i e h")).then_inc(ld["dn"], 16)

            def write_parts(g, j):
                sp.wait_ge(S_("part3"), 4 * g + ORDER.index(j) + 1)
                which, c = divmod(j, HC)
                for t in range(3):
                    dst = qk_dram[which, g * GT:(g + 1) * GT, c, t].rearrange("t d h n -> (d h) t n")
                    sp.dma_start(dst, parts[:, j, t, :].rearrange("p (t n) -> p t n", t=GT)).then_inc(S_("parts_written"), 16)

            def load_stack(b):
                sp.wait_ge(S_("parts_written"), 16 * 12 * (b // GT + 1))
                if b >= 3:
                    sp.wait_ge(S_("sT_ready"), NC * (b - 2))
                for n, part in enumerate(SLOTS_Q):
                    src = qk_dram[0, b, :, part].rearrange("c d h n -> d c (h n)")
                    dst = q_st[n * HD:(n + 1) * HD, b % 3, :, :].rearrange("p (c h) n -> p c (h n)", c=HC)
                    sp.dma_start(dst, src).then_inc(stack_loaded[b % 3], 16)
                for first, count in ((0, 3), (3, 2), (5, 1)):
                    src = qk_dram[1, b, :, 0:count].rearrange("c s d h n -> (s d) c (h n)")
                    dst = k_st[first * HD:(first + count) * HD, b % 3, :, :].rearrange("p (c h) n -> p c (h n)", c=HC)
                    sp.dma_start(dst, src).then_inc(stack_loaded[b % 3], 16)

            for g in range(NG):
                for j in ORDER:
                    write_parts(g, j)
                if g == 0:
                    for b in range(3):
                        load_stack(b)
            for b in range(NT):
                sp.wait_ge(S_("mT_copied"), b + 1)
                for t in range(3):
                    sp.dma_start(q_st[KS + t:KS + t + 1, b % 3, :, :], mT[t * NH:(t + 1) * NH, :]).then_inc(m_loaded[b % 2], 16)
                if b + 3 < NT:
                    load_stack(b + 3)
            for g in range(NG):
                for k in range(2):
                    sp.wait_ge(S_("out_ready"), 2 * g + k + 1)
                    t0 = g * GT + 2 * k
                    sp.dma_start(out_v[:, t0:t0 + 2, :], x_sb[:, t0:t0 + 2, :]).then_inc(S_("stored"), 16)
            sp.wait_ge(S_("stored"), 16 * 2 * NG)

        @block.gpsimd
        def _(pool):
            step = [0]

            def link(ins):
                step[0] += 1
                ins.then_inc(S_("pool_chain"), 1)
                pool.wait_ge(S_("pool_chain"), step[0])

            link(pool.memset(minus_half[:, :], -0.5))
            link(pool.memset(ident[:, :], 0.0))
            link(pool.affine_select(out=ident[:, :], in_=ident[:, :], compare_op=ALU.not_equal, fill=1.0,
                                    base=0, pattern=[[-1, P]], channel_multiplier=1))
            pool.tensor_copy(ident_b[:, :], ident[:, :]).then_inc(S_("ident_made"), 1)

            def normaliser(which, lo, hi, name, n):
                pool.wait_ge(S_(name), n)
                link(pool.tensor_scalar(var_eps[:, lo:hi], mv[:, which, lo:hi, 1], EPS, None, ALU.add))
                pool.tensor_tensor(rstd[:, which, lo:hi], var_eps[:, lo:hi], minus_half[:, lo:hi], ALU.pow)\
                    .then_inc(S_("rstd1_ready" if which == 0 else "rstd2_ready"), 1)

            normaliser(0, 0, GT, "mv1_ready", GT)
            link(pool.memset(expert_rows[:, :], 1.0))
            link(pool.affine_select(out=expert_rows[:, :], in_=expert_rows[:, :], compare_op=ALU.is_ge, fill=0.0,
                                    base=0, pattern=[[-R, E]], channel_multiplier=1))
            pool.affine_select(out=expert_rows[:, :], in_=expert_rows[:, :], compare_op=ALU.is_ge, fill=0.0,
                               base=R - 1, pattern=[[R, E]], channel_multiplier=-1).then_inc(S_("rows_made"), 1)
            normaliser(0, GT, NT, "mv1_ready", NT)
            link(pool.memset(causal[:, :, :], 0.0))
            pool.affine_select(out=causal[:, :, :], in_=causal[:, :, :], compare_op=ALU.is_ge, fill=MASKED,
                               base=0, pattern=[[0, 4], [-1, P]], channel_multiplier=1).then_inc(S_("causal_made"), 1)
            pool.wait_ge(S_("causal_made"), 1)
            pool.memset(k_st[KS:KM, :, :, :], 1.0).then_inc(S_("k_ones"), 1)
            pool.wait_ge(S_("k_ones"), 1)
            pool.memset(v_sb[:, :, :, HD:VW], 1.0).then_inc(S_("v_ones"), 1)
            pool.wait_ge(S_("v_ones"), 1)
            link(pool.memset(pick[:, :, :], 0.0))
            for t in range(3):
                link(pool.affine_select(out=pick[:, :, :], in_=pick[:, :, :], compare_op=ALU.not_equal, fill=1.0,
                                        base=-E * t, pattern=[[-1, E], [0, P]], channel_multiplier=1))
            link(pool.memset(earlier[:, :, :], 1.0))
            pool.affine_select(out=earlier[:, :, :], in_=earlier[:, :, :], compare_op=ALU.is_ge, fill=0.0,
                               base=-1, pattern=[[1, E], [-1, E]], channel_multiplier=0).then_inc(S_("router_consts"), 1)
            pool.wait_ge(S_("router_consts"), 1)

            for g in range(NG):
                for i, j in enumerate(ORDER):
                    pool.wait_ge(S_("part2"), 4 * g + i + 1)
                    if g:
                        pool.wait_ge(S_("parts_written"), 16 * 12 * g)
                    pool.tensor_tensor(parts[:, j, 2, :], rest[:, i % 2, :], parts[:, j, 1, :], ALU.subtract)\
                        .then_inc(S_("part3"), 1)
            pool.wait_ge(S_("parts_written"), 16 * 12 * NG)
            pool.wait_ge(S_("part3"), 4 * NG)
            pool.wait_ge(S_("v_proj"), 2 * NG)
            pool.wait_ge(S_("q_proj"), 2 * NG)

            def lows(n):
                if n < 4:
                    c, e0 = n // 2, (n % 2) * 4
                    pool.wait_ge(S_("up_hi_ready"), n + 1)
                    pool.tensor_tensor(up_lo[:, c, e0:e0 + 4, :], up_w[:, c, e0:e0 + 4, :],
                                       up_hi[:, c, e0:e0 + 4, :].bitcast(F32), ALU.subtract).then_inc(S_("lows_ready"), 1)
                elif n < 6:
                    e0 = (n - 4) * 4
                    pool.wait_ge(S_("dn_hi_ready"), n - 3)
                    pool.tensor_tensor(dn_lo[:, e0:e0 + 4, :], dn_w[:, e0:e0 + 4, :],
                                       dn_hi[:, e0:e0 + 4, :].bitcast(F32), ALU.subtract).then_inc(S_("lows_ready"), 1)

            for b in range(NT + 1):
                if b < NT:
                    for c in range(NC):
                        pool.wait_ge(S_("exp_done"), NC * b + c + 1)
                        ch = probsT[:, b % 2, 4 * c:4 * c + 4, :]
                        pool.affine_select(out=ch, in_=ch, compare_op=ALU.is_ge, fill=0.0, base=0,
                                           pattern=[[0, 4], [1, P]], channel_multiplier=-1).then_inc(S_("probs_ready"), 1)
                if b >= 1:
                    normaliser(1, b - 1, b, "mv2_ready", b)
                if b < NT:
                    lows(b)

        @block.scalar
        def _(act):
            def high(out_, in_, done, scale=1.0):
                act.activation(out_, in_, ACT.Copy, scale=scale).then_inc(S_(done), 1)

            act.wait_ge(S_("wkv_T"), 1)
            high(wkv_hi[:, 0:H].rearrange("p (a d h) -> p a h d", a=HC, d=HD),
                 bank[3][:, 0:H].rearrange("p (a h d) -> p a h d", a=HC, d=HD), "wkv_hi_ready")
            high(wkv_hi[:, H:2 * H], bank[3][:, H:2 * H], "wkv_hi_ready")
            act.wait_ge(S_("wq_T"), 1)
            for ic in range(HC):
                high(wqT_hi[:, ic, :].rearrange("p (a d h) -> p a h d", a=HC, d=HD),
                     bank[2][:, ic * H:(ic + 1) * H].rearrange("p (a h d) -> p a h d", a=HC, d=HD), "wq_hi_ready", SCALE)
            for g in range(NG):
                act.wait_ge(S_("c_T"), g + 1)
                if g:
                    act.wait_ge(S_("v_proj"), 2 * g)
                    act.wait_ge(S_("cT_lo"), g)
                high(cT[0:L, :], bank[4][0:L, :], "cT_hi")
                high(cT_tmp[L:P, :], bank[4][L:P, :], "cT_hi")
                for ic in range(HC):
                    act.wait_ge(S_("x_T"), HC * g + ic + 1)
                    high(xT_hi[:, ic, xT_src(g)], bank[ic][:, :], "xT_hi_ready")
                for k in range(2):
                    act.wait_ge(S_("v_proj"), 2 * g + k + 1)
                    t0 = g * GT + 2 * k
                    high(v_sb[:, t0:t0 + 2, :, 0:HD],
                         bank[3 + k][:, :].rearrange("p (t h d) -> p t h d", t=2, d=HD), "v_ready")
                for i, j in enumerate(ORDER):
                    act.wait_ge(S_("q_proj" if j < HC else "k_proj"), HC * g + j % HC + 1)
                    if g:
                        act.wait_ge(S_("parts_written"), 16 * 12 * g)
                    high(parts[:, j, 0, :], QK_BANK(j)[:, :], "part1")
                    if i:
                        act.wait_ge(S_("rest_ready"), 4 * g + i)
                        high(parts[:, ORDER[i - 1], 1, :], rest[:, (i - 1) % 2, :], "part2")
                act.wait_ge(S_("rest_ready"), 4 * g + 4)
                high(parts[:, ORDER[3], 1, :], rest[:, 1, :], "part2")
            act.wait_ge(S_("lora_T"), 1)
            high(loraBT[:, :, :].rearrange("p a n -> p (a n)"), bank[1][:, :], "lora_ready", LORA)
            act.wait_ge(S_("gb_T"), 1)
            high(gbT[:, :], bank[2][0:R, 0:E], "gbT_ready", LORA)
            act.wait_ge(S_("wo_T"), 1)
            high(woT_hi[:, :, :].rearrange("p a n -> p (a n)"), bank[0][:, :], "wo_hi_ready")
            act.wait_ge(S_("wr_T"), 1)
            act.wait_ge(S_("wr_zero"), 2)
            high(wr_hi[:, :, 0:E], bank[3][:, 0:HC * E].rearrange("p (a e) -> p a e", a=HC), "wr_hi_ready")

            def expert_highs(n):
                if n < 4:
                    c, e0 = n // 2, (n % 2) * 4
                    act.wait_ge(S_("up_merged"), (n + 1) * 2)
                    high(up_hi[:, c, e0:e0 + 4, :], up_w[:, c, e0:e0 + 4, :], "up_hi_ready")
                elif n < 6:
                    e0 = (n - 4) * 4
                    act.wait_ge(S_("dn_merged"), (n - 3) * 2)
                    high(dn_hi[:, e0:e0 + 4, :], dn_w[:, e0:e0 + 4, :], "dn_hi_ready")

            def mT_copy(b):
                act.wait_ge(S_("mT_ready"), b + 1)
                if b:
                    act.wait_ge(m_loaded[(b - 1) % 2], 48 * ((b - 1) // 2 + 1))
                act.activation(mT[:, :], bank[5][0:3 * NH, 0:P // 2].bitcast(BF16), ACT.Copy).then_inc(S_("mT_copied"), 1)

            def exp_chunk(b, c):
                act.wait_ge(S_("sT_ready"), NC * b + c + 1)
                if b >= 2 and c == 0:
                    act.wait_ge(S_("pv_done"), b - 1)
                if b == 0 and c == 0:
                    act.wait_ge(S_("up_lora"), HC * E // 2)
                    act.wait_ge(S_("dn_lora"), E // 2)
                act.activation(probsT[:, b % 2, 4 * c:4 * c + 4, :].rearrange("p h n -> p (h n)"),
                               bank[2 + c % 2][:, :], ACT.Exp).then_inc(S_("exp_done"), 1)

            mT_copy(0)
            for b in range(NT + 1):
                if b < NT:
                    exp_chunk(b, 0)
                    exp_chunk(b, 1)
                if b >= 1:
                    act.wait_ge(S_("o_T"), b)
                    if b >= 2:
                        act.wait_ge(S_("o_out"), b - 1)
                    high(oT_hi[:, :, :].rearrange("p a n -> p (a n)"), bank[6][:, 0:HC * P], "oT_hi_ready")
                if b < NT:
                    exp_chunk(b, 2)
                    exp_chunk(b, 3)
                    if b + 1 < NT:
                        mT_copy(b + 1)
                    act.wait_ge(S_("pv_done"), b + 1)
                    if b:
                        act.wait_ge(S_("on_ready"), b)
                    high(oT_sb[:, :, :].rearrange("p a n -> p (a n)"), bank[4][:, :], "oT_copied")
                if b >= 1:
                    act.wait_ge(S_("x2_T"), b)
                    high(xT_hi[:, :, (b - 1) * P:b * P], bank[6][:, HC * P:2 * HC * P].rearrange("p (a n) -> p a n", a=HC), "x2T_hi")
                if b < NT:
                    expert_highs(b)
                for g, first in enumerate(ROUTER_AT):
                    if b == first:
                        act.wait_ge(S_("lgT_ready"), g + 1)
                        high(lgT[:, :], bank[7][0:E, :], "lgT_copied")
                    if b == first + 1:
                        act.wait_ge(S_("lsub_ready"), g + 1)
                        act.activation(lexp[:, :, :], lsub[:, :, :], ACT.Exp).then_inc(S_("lexp_ready"), 1)
                    if b == first + 2:
                        act.wait_ge(S_("wT_ready"), g + 1)
                        act.activation(wT[:, g, :], bank[5][0:3 * E, 0:GN // 2].bitcast(BF16), ACT.Copy).then_inc(S_("wT_copied"), 1)
            act.wait_ge(S_("lgT_ready"), NG)
            high(lgT[:, :], bank[5][0:E, :], "lgT_copied")
            act.wait_ge(S_("lsub_ready"), NG)
            act.activation(lexp[:, :, :], lsub[:, :, :], ACT.Exp).then_inc(S_("lexp_ready"), 1)
            act.wait_ge(S_("wT_ready"), NG)
            act.activation(wT[:, NG - 1, :], bank[5][0:3 * E, 0:GN // 2].bitcast(BF16), ACT.Copy).then_inc(S_("wT_copied"), 1)

            act.wait_ge(S_("lows_ready"), 6)
            for n in range(NG * E):
                k = n % 2
                act.wait_ge(S_("gate_ready"), n + 1)
                if n >= 2:
                    act.wait_ge(S_("gated_ready"), n - 1)
                act.activation(silu[:, k, :], bank[k][:, :], ACT.Silu).then_inc(S_("silu_ready"), 1)
                act.wait_ge(S_("h_ready"), n + 1)
                if n >= 2:
                    act.wait_ge(S_("down_done"), n - 1)
                high(h_hi[:, k, :], h_f[:, k, :], "h_hi_ready")

        @block.vector
        def _(dve):
            step = [0]

            def link(ins):
                step[0] += 1
                ins.then_inc(S_("dve_chain"), 1)
                dve.wait_ge(S_("dve_chain"), step[0])

            def low(out_, in_, hi, done, scale=1.0):
                dve.scalar_tensor_tensor(out=out_, in0=in_, scalar=scale, in1=hi.bitcast(F32), op0=ALU.mult,
                                         op1=ALU.subtract).then_inc(S_(done), 1)

            def norm_stats(which, t, done, src=None):
                link(dve.bn_stats(stats[:, which, t, :], x_sb[:, t, :]))
                dve.bn_aggr(mv[:, which, t, :], stats[:, which, t, :]).then_inc(S_(done), 1)

            def normalise(which, t, out_, done):
                dve.tensor_scalar(out_, x_sb[:, t, :], mv[:, which, t, 0:1], rstd[:, which, t:t + 1],
                                  ALU.subtract, ALU.mult).then_inc(S_(done), 1)

            dve.memset(wkv_lo[L:P, :].bitcast(F32), 0.0).then_inc(S_("wkv_zero"), 1)
            dve.memset(wr_hi[:, :, :].bitcast(F32), 0.0).then_inc(S_("wr_zero"), 1)
            dve.memset(wr_lo[:, :, :].bitcast(F32), 0.0).then_inc(S_("wr_zero"), 1)
            for g in range(NG):
                if g == 0:
                    dve.wait_ge(ld["x0"], 16)
                    for t in range(GT):
                        norm_stats(0, t, "mv1_ready")
                    dve.wait_ge(S_("wkv_hi_ready"), 2)
                    for a in range(HC):
                        cols = slice(a * P, (a + 1) * P)
                        low(wkv_lo[0:L, cols].rearrange("p (d h) -> p h d", d=HD),
                            bank[3][0:L, cols].rearrange("p (h d) -> p h d", d=HD),
                            wkv_hi[0:L, cols].rearrange("p (d h) -> p h d", d=HD), "wkv_lo_ready")
                    low(wkv_lo[0:L, H:2 * H], bank[3][0:L, H:2 * H], wkv_hi[0:L, H:2 * H], "wkv_lo_ready")
                dve.wait_ge(S_("rstd1_ready"), g + 1)
                if g:
                    dve.wait_ge(S_("x_T"), HC * g)
                for t in range(GT):
                    normalise(0, g * GT + t, xhat[:, t, :], "xhat_ready")
                if g + 1 < NG:
                    dve.wait_ge(ld["x1"], 16)
                    for t in range((g + 1) * GT, (g + 2) * GT):
                        norm_stats(0, t, "mv1_ready")
                if g == 0:
                    dve.wait_ge(S_("wq_hi_ready"), 2)
                    for ic in range(HC):
                        for a in range(HC):
                            cols = slice(a * P, (a + 1) * P)
                            low(wqT_lo[:, ic, cols].rearrange("p (d h) -> p h d", d=HD),
                                bank[2][:, ic * H + a * P:ic * H + (a + 1) * P].rearrange("p (h d) -> p h d", d=HD),
                                wqT_hi[:, ic, cols].rearrange("p (d h) -> p h d", d=HD), "wq_lo_ready", SCALE)
                dve.wait_ge(S_("cT_hi"), 2 * (g + 1))
                low(cT[L:P, :], bank[4][L:P, :], cT_tmp[L:P, :], "cT_lo")
                for ic in range(HC):
                    dve.wait_ge(S_("xT_hi_ready"), HC * g + ic + 1)
                    low(xT_lo[:, ic, xT_src(g)], bank[ic][:, :], xT_hi[:, ic, xT_src(g)], "xT_lo_ready")
                for i, j in enumerate(ORDER):
                    dve.wait_ge(S_("part1"), 4 * g + i + 1)
                    if 4 * g + i >= 2:
                        dve.wait_ge(S_("part3"), 4 * g + i - 1)
                    dve.tensor_tensor(rest[:, i % 2, :], QK_BANK(j)[:, :], parts[:, j, 0, :], ALU.subtract)\
                        .then_inc(S_("rest_ready"), 1)
            dve.wait_ge(S_("rows_made"), 1)
            dve.wait_ge(ld["upA"], 16)
            dve.wait_ge(ld["dnA"], 16)
            dve.tensor_tensor(upA_bd, upA_raw[:, None, :].to_broadcast([P, E, H]),
                              expert_rows[:, :, None].to_broadcast([P, E, H]), ALU.mult).then_inc(S_("upA_spread"), 1)
            dve.tensor_tensor(dnA_bd, dnA_raw[:, None, :].to_broadcast([P, E, I]),
                              expert_rows[:, :, None].to_broadcast([P, E, I]), ALU.mult).then_inc(S_("dnA_spread"), 1)
            dve.wait_ge(S_("wo_hi_ready"), 1)
            low(woT_lo[:, :, :].rearrange("p a n -> p (a n)"), bank[0][:, :],
                woT_hi[:, :, :].rearrange("p a n -> p (a n)"), "wo_lo_ready")
            dve.wait_ge(S_("wr_hi_ready"), 1)
            low(wr_lo[:, :, 0:E], bank[3][:, 0:HC * E].rearrange("p (a e) -> p a e", a=HC), wr_hi[:, :, 0:E], "wr_lo_ready")
            dve.wait_ge(S_("o_bank_free"), 1)
            dve.memset(bank[4][:, :], 0.0).then_inc(S_("o_zero"), 1)
            dve.wait_ge(ld["up"], 32)
            for n in range(HC * E // 2):
                c, e0 = divmod(2 * n, E)
                dve.wait_ge(S_("up_lora"), n + 1)
                dve.tensor_tensor(up_w[:, c, e0:e0 + 2, :], bank[LORA_BANK(n)][:, :].rearrange("p (e n) -> p e n", e=2),
                                  up_w[:, c, e0:e0 + 2, :], ALU.add).then_inc(S_("up_merged"), 1)
            dve.wait_ge(ld["dn"], 16)
            for n in range(E // 2):
                dve.wait_ge(S_("dn_lora"), n + 1)
                dve.tensor_tensor(dn_w[:, 2 * n:2 * n + 2, :], bank[LORA_BANK(n)][:, :].rearrange("p (e n) -> p e n", e=2),
                                  dn_w[:, 2 * n:2 * n + 2, :], ALU.add).then_inc(S_("dn_merged"), 1)

            def max_chunk(b, c):
                dve.wait_ge(S_("s_ready"), NC * b + c + 1)
                dve.reduce_max(m_sb[:, b % 2, 4 * c:4 * c + 4], bank[c % 2][:, :].rearrange("p (h n) -> p h n", h=4), AX.X)\
                    .then_inc(S_("max_done"), 1)

            def max_parts(b):
                m = m_sb[:, b % 2, :]
                dve.wait_ge(S_("max_done"), NC * (b + 1))
                if b:
                    dve.wait_ge(S_("mT_ready"), b)
                link(dve.tensor_scalar(m_parts[:, 0, :], m, -1.0, None, ALU.mult))
                link(dve.scalar_tensor_tensor(out=m_rest[:, :], in0=m, scalar=-1.0, in1=m_parts[:, 0, :],
                                              op0=ALU.mult, op1=ALU.subtract))
                link(dve.tensor_copy(m_parts[:, 1, :], m_rest[:, :]))
                dve.tensor_tensor(m_parts[:, 2, :], m_rest[:, :], m_parts[:, 1, :], ALU.subtract)\
                    .then_inc(S_("m_parts_ready"), 1)

            def route(g, lg_bank):
                dve.wait_ge(S_("lg_ready"), g + 1)
                link(dve.tensor_copy(lg[:, :, :], lg_bank[:, 0:GT * E].rearrange("p (t e) -> p t e", e=E)))
                link(dve.reduce_max(lmax[:, :], lg[:, :, :], AX.X))
                dve.tensor_tensor(lsub[:, :, :], lg[:, :, :], lmax[:, :, None].to_broadcast([P, GT, E]), ALU.subtract)\
                    .then_inc(S_("lsub_ready"), 1)
                other = lg[:, :, None, :].to_broadcast([P, GT, E, E])
                mine = lg[:, :, :, None].to_broadcast([P, GT, E, E])
                for t in range(GT):
                    link(dve.tensor_tensor(above[:, t], other[:, t], mine[:, t], ALU.is_gt))
                    link(dve.tensor_tensor(equal[:, t], other[:, t], mine[:, t], ALU.is_equal))
                    link(dve.tensor_tensor(equal[:, t], equal[:, t], earlier[:, :, :], ALU.mult))
                    link(dve.tensor_tensor(above[:, t], above[:, t], equal[:, t], ALU.add))
                    link(dve.reduce_sum(rank[:, t, :], above[:, t], AX.X))
                link(dve.tensor_scalar(chosen[:, :, :], rank[:, :, :], 1.5, None, ALU.is_lt))
                dve.wait_ge(S_("lexp_ready"), g + 1)
                link(dve.tensor_tensor(lpick[:, :, :], lexp[:, :, :], chosen[:, :, :], ALU.mult))
                link(dve.reduce_sum(lsum[:, :], lpick[:, :, :], AX.X))
                link(dve.reciprocal(linv[:, :], lsum[:, :]))
                link(dve.tensor_tensor(wts[:, :, :], lpick[:, :, :], linv[:, :, None].to_broadcast([P, GT, E]), ALU.mult))
                link(dve.tensor_copy(w_parts[:, :, 0, :], wts[:, :, :]))
                link(dve.tensor_tensor(w_rest[:, :, :], wts[:, :, :], w_parts[:, :, 0, :], ALU.subtract))
                link(dve.tensor_copy(w_parts[:, :, 1, :], w_rest[:, :, :]))
                dve.tensor_tensor(w_parts[:, :, 2, :], w_rest[:, :, :], w_parts[:, :, 1, :], ALU.subtract)\
                    .then_inc(S_("w_parts_ready"), 1)

            for c in range(NC):
                max_chunk(0, c)
            max_parts(0)
            dve.wait_ge(S_("router_consts"), 1)
            for b in range(NT + 1):
                if b + 1 < NT:
                    max_chunk(b + 1, 0)
                    max_chunk(b + 1, 1)
                if b >= 1:
                    dve.wait_ge(S_("on_ready"), b)
                    on = bank[5][:, :].rearrange("p (c j w) -> p c j w", c=4, j=4)
                    link(dve.reciprocal(r_den[:, :, :], on[:, :, :, HD]))
                    o4 = o_nat[:, :, :].rearrange("p (c j) d -> p c j d", c=4)
                    for c in range(4):
                        last = dve.tensor_tensor(o4[:, c], on[:, c, :, 0:HD],
                                                 r_den[:, c, :, None].to_broadcast([P, 4, HD]), ALU.mult)
                        last.then_inc(S_("o_nat_ready"), 1)
                    dve.wait_ge(S_("oT_hi_ready"), b)
                    low(oT_lo[:, :, :].rearrange("p a n -> p (a n)"), bank[6][:, 0:HC * P],
                        oT_hi[:, :, :].rearrange("p a n -> p (a n)"), "oT_lo_ready")
                if b + 1 < NT:
                    max_chunk(b + 1, 2)
                    max_chunk(b + 1, 3)
                    max_parts(b + 1)
                if b >= 1:
                    t = b - 1
                    dve.wait_ge(S_("o_out"), b)
                    link(dve.tensor_tensor(x_sb[:, t, :], bank[7][:, 0:H], x_sb[:, t, :], ALU.add))
                    norm_stats(1, t, "mv2_ready")
                    dve.wait_ge(S_("rstd2_ready"), b)
                    if b >= 2:
                        dve.wait_ge(S_("x2_T"), b - 1)
                    normalise(1, t, x2hat[:, :], "x2hat_ready")
                    dve.wait_ge(S_("x2T_hi"), b)
                    low(xT_lo[:, :, t * P:(t + 1) * P], bank[6][:, HC * P:2 * HC * P].rearrange("p (a n) -> p a n", a=HC),
                        xT_hi[:, :, t * P:(t + 1) * P], "x2T_lo")
                for g, first in enumerate(ROUTER_AT):
                    if b == first + 1:
                        route(g, bank[5])
            route(NG - 1, bank[5])

            dve.wait_ge(S_("lows_ready"), 6)
            for n in range(NG * E):
                g, e = divmod(n, E)
                k = n % 2
                dve.wait_ge(S_("silu_ready"), n + 1)
                dve.wait_ge(S_("up_ready"), n + 1)
                dve.tensor_tensor(gated[:, k, :], bank[2 + k][:, :], silu[:, k, :], ALU.mult).then_inc(S_("gated_ready"), 1)
                dve.wait_ge(S_("gated_ready"), n + 1)
                dve.wait_ge(S_("weight_ready"), n + 1)
                dve.tensor_tensor(h_f[:, k, :], bank[4][:, :], gated[:, k, :], ALU.mult).then_inc(S_("h_ready"), 1)
                dve.wait_ge(S_("h_hi_ready"), n + 1)
                dve.tensor_tensor(h_lo[:, k, :], h_f[:, k, :], h_hi[:, k, :].bitcast(F32), ALU.subtract)\
                    .then_inc(S_("h_lo_ready"), 1)
                if e == E - 1:
                    dve.wait_ge(S_("down_done"), n + 1)
                    for k2 in range(2):
                        t0 = g * GT + 2 * k2
                        dve.tensor_tensor(x_sb[:, t0:t0 + 2, :], bank[6 + k2][:, :].rearrange("p (t n) -> p t n", t=2),
                                          x_sb[:, t0:t0 + 2, :], ALU.add).then_inc(S_("out_ready"), 1)

        @block.tensor
        def _(pe):
            def products(out_, pairs, done=None, start=True, stop=True, **kw):
                for i, (a, m) in enumerate(pairs):
                    last = pe.matmul(out_, a, m, start=start and i == 0, stop=stop and i == len(pairs) - 1, **kw)
                if done:
                    last.then_inc(S_(done), 1)

            pe.wait_ge(S_("ident_made"), 1)
            pe.wait_ge(ld["wkv"], 32)
            for oc in range(4):
                last = pe.transpose(bank[3][:, oc * P:(oc + 1) * P], wkv_raw[:, oc, :, :].rearrange("p k l -> p (k l)"), ident[:, :])
            last.then_inc(S_("wkv_T"), 1)

            def context_T(g):
                if g == 0:
                    pe.wait_ge(ld["ctx"], 32)
                else:
                    pe.wait_ge(S_("v_ready"), 2 * g)
                for t in range(GT):
                    last = pe.transpose(bank[4][:, t * P:(t + 1) * P],
                                        ctx_sb[:, g * GT + t, :, :].rearrange("p k l -> p (k l)"), ident[:, :])
                last.then_inc(S_("c_T"), 1)

            def x_T(g):
                pe.wait_ge(S_("xhat_ready"), GT * (g + 1))
                if g:
                    pe.wait_ge(S_("xT_lo_ready"), HC * g)
                for ic in range(HC):
                    for t in range(GT):
                        last = pe.transpose(bank[ic][:, t * P:(t + 1) * P], xhat[:, t, ic * P:(ic + 1) * P], ident[:, :])
                    last.then_inc(S_("x_T"), 1)

            def kv_proj(g):
                pe.wait_ge(S_("wkv_lo_ready"), HC + 1)
                pe.wait_ge(S_("wkv_zero"), 1)
                pe.wait_ge(S_("wkv_hi_ready"), 2)
                pe.wait_ge(S_("wq_lo_ready"), HC * HC)
                pe.wait_ge(S_("cT_lo"), g + 1)
                if g:
                    pe.wait_ge(S_("rest_ready"), 4 * g)
                    pe.wait_ge(S_("v_ready"), 2 * g)
                for oc in range(HC):
                    cols = slice(oc * P, (oc + 1) * P)
                    products(QK_BANK(HC + oc)[:, :], [(wkv_hi[:, cols], cT[:, :]), (wkv_lo[:, cols], cT[:, :])], "k_proj")
                for k in range(2):
                    for t in range(2):
                        tok = slice((2 * k + t) * P, (2 * k + t + 1) * P)
                        products(bank[3 + k][:, t * H:(t + 1) * H],
                                 [(cT[:, tok], wkv_hi[:, H:2 * H]), (cT[:, tok], wkv_lo[:, H:2 * H])],
                                 "v_proj" if t else None)

            def q_proj(g):
                pe.wait_ge(S_("xT_lo_ready"), HC * (g + 1))
                for oc in range(HC):
                    cols = slice(oc * P, (oc + 1) * P)
                    products(QK_BANK(oc)[:, :],
                             [(w[:, ic, cols], xt[:, ic, xT_src(g)]) for ic in range(HC)
                              for w, xt in ((wqT_hi, xT_hi), (wqT_hi, xT_lo), (wqT_lo, xT_hi))], "q_proj")

            pe.wait_ge(ld["wq"], 16)
            for ic in range(HC):
                for oc in range(HC):
                    last = pe.transpose(bank[2][:, ic * H + oc * P:ic * H + (oc + 1) * P],
                                        wq_raw[:, oc, ic * P:(ic + 1) * P], ident[:, :])
            last.then_inc(S_("wq_T"), 1)
            for g in range(NG):
                context_T(g)
                x_T(g)
                kv_proj(g)
                q_proj(g)

            pe.wait_ge(ld["upB"], 32)
            pe.wait_ge(ld["dnB"], 32)
            pe.wait_ge(S_("xT_lo_ready"), HC * NG)
            for k, raw in enumerate((upB_raw, dnB_raw)):
                for c in range(HC):
                    last = pe.transpose(bank[1][:, k * H + c * P:k * H + (c + 1) * P],
                                        raw[:, c, :, :].rearrange("p e r -> p (e r)"), ident[:, :])
            last.then_inc(S_("lora_T"), 1)
            pe.wait_ge(ld["gate"], 48)
            pe.wait_ge(S_("rest_ready"), 4 * NG)
            pe.transpose(bank[2][0:R, 0:E], gb_raw[:, :], ident[0:E, 0:E]).then_inc(S_("gb_T"), 1)
            pe.wait_ge(ld["wo"], 16)
            for ic in range(HC):
                for oc in range(HC):
                    last = pe.transpose(bank[0][:, ic * H + oc * P:ic * H + (oc + 1) * P],
                                        wo_raw[:, oc, ic * P:(ic + 1) * P], ident[:, :])
            last.then_inc(S_("wo_T"), 1)
            pe.wait_ge(S_("v_ready"), 2 * NG)
            pe.wait_ge(S_("gbT_ready"), 1)
            for ic in range(HC):
                products(bank[3][:, ic * E:(ic + 1) * E],
                         [(gw_raw[:, ic * P:(ic + 1) * P], ident[0:E, 0:E]), (ga_raw[:, ic * P:(ic + 1) * P], gbT[:, :])],
                         "wr_T" if ic else None)
            pe.wait_ge(S_("lora_ready"), 1)
            pe.wait_ge(S_("upA_spread"), 1)
            pe.matmul(bank[4][0:E, 0:E], gw_raw[:, 0:E], ident[0:E, 0:E], start=True, stop=True).then_inc(S_("o_bank_free"), 1)
            for n in range(HC * E // 2):
                c, e0 = divmod(2 * n, E)
                if n >= 3:
                    pe.wait_ge(S_("up_merged"), n - 2)
                for k in range(2):
                    products(bank[LORA_BANK(n)][:, k * H:(k + 1) * H],
                             [(upA_bd[:, e0 + k, c * P:(c + 1) * P], loraBT[:, 0, :])], "up_lora" if k else None)
            pe.wait_ge(S_("dnA_spread"), 1)
            for n in range(E // 2):
                pe.wait_ge(S_("up_merged"), min(HC * E // 2, HC * E // 2 - 1 + n))
                if n >= 3:
                    pe.wait_ge(S_("dn_merged"), n - 2)
                for k in range(2):
                    products(bank[LORA_BANK(n)][:, k * H:(k + 1) * H],
                             [(dnA_bd[:, 2 * n + k, :], loraBT[:, 1, :])], "dn_lora" if k else None)

            def s_chunk(b, c):
                n = NC * b + c
                if c == 0:
                    pe.wait_ge(stack_loaded[b % 3], 16 * 9 * (b // 3 + 1))
                if n >= 2:
                    pe.wait_ge(S_("max_done"), n - 1)
                pe.matmul(bank[c % 2][:, :], ident_b[:, :], causal[:, :, :].rearrange("p h n -> p (h n)"),
                          start=True, stop=True, skip_group_check=True)
                for j in range(4):
                    h = 4 * c + j
                    last = pe.matmul(bank[c % 2][:, j * P:(j + 1) * P], q_st[0:KS, b % 3, h, :], k_st[0:KS, b % 3, h, :],
                                     start=False, stop=True, skip_group_check=True)
                last.then_inc(S_("s_ready"), 1)

            def sT_chunk(b, c):
                n = NC * b + c
                if c == 0:
                    pe.wait_ge(m_loaded[b % 2], 48 * (b // 2 + 1))
                if n >= 2:
                    pe.wait_ge(S_("exp_done"), n - 1)
                for j in range(4):
                    h = 4 * c + j
                    last = pe.matmul(bank[2 + c % 2][:, j * P:(j + 1) * P], k_st[0:KM, b % 3, h, :], q_st[0:KM, b % 3, h, :],
                                     start=True, stop=True)
                last.then_inc(S_("sT_ready"), 1)

            def max_T(b):
                pe.wait_ge(S_("m_parts_ready"), b + 1)
                pe.transpose(bank[5][0:3 * NH, 0:P // 2].bitcast(BF16), m_parts[:, :, :].rearrange("p t h -> p (t h)"),
                             ident_b[:, :]).then_inc(S_("mT_ready"), 1)

            def lgT(g, bk):
                pe.wait_ge(S_("x2T_lo"), GT * (g + 1))
                products(bk[:, :], [(w[:, ic, :], xt[:, ic, xT_src(g)]) for ic in range(HC)
                                    for w, xt in ((wr_hi, xT_hi), (wr_hi, xT_lo), (wr_lo, xT_hi))], "lgT_ready")

            def lg_T(g):
                pe.wait_ge(S_("lgT_copied"), g + 1)
                for t in range(GT):
                    last = pe.transpose(bank[5][:, t * E:(t + 1) * E], lgT_rows[:, t * P:(t + 1) * P], ident[0:E, 0:E])
                last.then_inc(S_("lg_ready"), 1)

            def w_T(g):
                pe.wait_ge(S_("w_parts_ready"), g + 1)
                for t in range(GT):
                    last = pe.transpose(bank[5][0:3 * E, t * P // 2:(t + 1) * P // 2].bitcast(BF16),
                                        w_parts[:, t, :, :].rearrange("p k e -> p (k e)"), ident_b[:, :])
                last.then_inc(S_("wT_ready"), 1)

            pe.wait_ge(S_("up_merged"), HC * E // 2)
            pe.wait_ge(S_("dn_merged"), E // 2)
            pe.wait_ge(S_("wo_lo_ready"), 1)
            pe.wait_ge(S_("wr_lo_ready"), 1)
            pe.wait_ge(S_("causal_made"), 1)
            pe.wait_ge(S_("k_ones"), 1)
            pe.wait_ge(S_("v_ones"), 1)
            pe.wait_ge(S_("o_zero"), 1)
            for c in range(NC):
                s_chunk(0, c)
            max_T(0)
            for b in range(NT + 1):
                if b + 1 < NT:
                    s_chunk(b + 1, 0)
                    s_chunk(b + 1, 1)
                if b >= 1:
                    pe.wait_ge(S_("oT_copied"), b)
                    if b < NT:
                        pe.wait_ge(S_("mT_copied"), b + 1)
                    for g, first in enumerate(ROUTER_AT):
                        if b == first + 2:
                            pe.wait_ge(S_("lsub_ready"), g + 1)
                        if b == first + 3:
                            pe.wait_ge(S_("wT_copied"), g + 1)
                    for c in range(4):
                        last = pe.transpose(bank[5][:, c * P:(c + 1) * P], oT_sb[:, c, :], ident[:, :])
                    last.then_inc(S_("on_ready"), 1)
                if b < NT:
                    sT_chunk(b, 0)
                    sT_chunk(b, 1)
                if b >= 1:
                    pe.wait_ge(S_("o_nat_ready"), 4 * b)
                    if b >= 2:
                        pe.wait_ge(S_("x2T_lo"), b - 1)
                    for ic in range(HC):
                        last = pe.transpose(bank[6][:, ic * P:(ic + 1) * P],
                                            o_nat[:, :, :].rearrange("p h d -> p (h d)")[:, ic * P:(ic + 1) * P], ident[:, :])
                    last.then_inc(S_("o_T"), 1)
                if b < NT:
                    sT_chunk(b, 2)
                    sT_chunk(b, 3)
                if b + 1 < NT:
                    s_chunk(b + 1, 2)
                    s_chunk(b + 1, 3)
                if b >= 1:
                    pe.wait_ge(S_("oT_lo_ready"), b)
                    if b - 1 in ROUTER_AT:
                        pe.wait_ge(S_("lgT_copied"), ROUTER_AT.index(b - 1) + 1)
                    products(bank[7][:, 0:H], [(a[:, ic, :], w[:, ic, :]) for ic in range(HC)
                                               for a, w in ((oT_hi, woT_hi), (oT_hi, woT_lo), (oT_lo, woT_hi))], "o_out")
                if b + 1 < NT:
                    max_T(b + 1)
                if b < NT:
                    for h in range(NH):
                        c, j = divmod(h, 4)
                        if j == 0:
                            pe.wait_ge(S_("probs_ready"), NC * b + c + 1)
                        if h == 0 and b:
                            pe.wait_ge(S_("oT_copied"), b)
                        last = pe.matmul(bank[4][32 * j:32 * j + VW, c * P:(c + 1) * P], v_sb[:, b, h, :],
                                         probsT[:, b % 2, h, :], start=True, stop=True)
                    last.then_inc(S_("pv_done"), 1)
                if b >= 1:
                    pe.wait_ge(S_("x2hat_ready"), b)
                    for ic in range(HC):
                        last = pe.transpose(bank[6][:, (HC + ic) * P:(HC + ic + 1) * P], x2hat[:, ic * P:(ic + 1) * P], ident[:, :])
                    last.then_inc(S_("x2_T"), 1)
                for g, first in enumerate(ROUTER_AT):
                    if b == first:
                        lgT(g, bank[7])
                    if b == first + 1:
                        if b + 1 < NT:
                            pe.wait_ge(S_("mT_copied"), b + 2)
                        lg_T(g)
                    if b == first + 2:
                        w_T(g)

            def gate_up_step(n):
                g, e = divmod(n, E)
                if n >= 2:
                    pe.wait_ge(S_("silu_ready"), n - 1)
                for name, half, base in (("gate_ready", 0, 0), ("up_ready", 1, 2)):
                    if n >= 2 and half:
                        pe.wait_ge(S_("gated_ready"), n - 1)
                    cols = slice(half * I, (half + 1) * I)
                    products(bank[base + n % 2][:, :],
                             [(w[:, ic, e, cols], xt[:, ic, xT_src(g)]) for ic in range(HC)
                              for w, xt in ((up_hi, xT_hi), (up_hi, xT_lo), (up_lo, xT_hi))], name)

            def weight_step(n):
                g, e = divmod(n, E)
                if e == 0:
                    pe.wait_ge(S_("wT_copied"), g + 1)
                if n:
                    pe.wait_ge(S_("h_ready"), n)
                products(bank[4][:, :], [(pick[:, e, :], wT[:, g, :])], "weight_ready")

            def down_step(n):
                g, e = divmod(n, E)
                k = n % 2
                pe.wait_ge(S_("h_lo_ready"), n + 1)
                if e == 0 and g:
                    pe.wait_ge(S_("out_ready"), 2 * g)
                for t in range(GT):
                    tok = slice(t * P, (t + 1) * P)
                    for i, (a, w) in enumerate(((h_hi, dn_hi), (h_hi, dn_lo), (h_lo, dn_hi))):
                        last = pe.matmul(bank[6 + t // 2][:, (t % 2) * H:(t % 2 + 1) * H], a[:, k, tok], w[:, e, :],
                                         start=e == 0 and t % 2 == 0 and i == 0, stop=e == E - 1 and i == 2,
                                         skip_group_check=True)
                last.then_inc(S_("down_done"), 1)

            pe.wait_ge(S_("lows_ready"), 6)
            pe.wait_ge(S_("x2T_lo"), NT)
            pe.wait_ge(S_("exp_done"), NC * NT)
            gate_up_step(0)
            lgT(NG - 1, bank[5])
            gate_up_step(1)
            lg_T(NG - 1)
            w_T(NG - 1)
            weight_step(0)
            for n in range(NG * E):
                if n >= 1 and n + 1 < NG * E:
                    gate_up_step(n + 1)
                down_step(n)
                if n + 1 < NG * E:
                    weight_step(n + 1)


_INS = ["x", "ctx_512", "L0_xattn_Wq", "L0_xattn_Wkv_expand", "L0_xattn_Wout", "L0_ffn_gate_weight",
        "L0_ffn_gate_lora_A", "L0_ffn_gate_lora_B", "L0_ffn_gate_up_proj", "L0_ffn_down_proj",
        "L0_ffn_gup_lora_A", "L0_ffn_gup_lora_B", "L0_ffn_down_lora_A", "L0_ffn_down_lora_B"]
_OUT = ((8, 128, 256), "float32")


def kernel(**inputs):
    import numpy as _np
    import concourse.bacc as _bacc
    from concourse import mybir as _mybir
    from concourse.bass_utils import run_bass_kernel_spmd as _run

    nc = _bacc.Bacc("TRN2", target_bir_lowering=False, num_devices=1)
    arrays, args = {}, []
    for name in _INS:
        a = _np.ascontiguousarray(inputs[name])
        arrays[f"in_{name}"] = a
        args.append(nc.dram_tensor(f"in_{name}", a.shape, _mybir.dt.from_np(a.dtype), kind="ExternalInput").ap())
    args.append(nc.dram_tensor("out_0", _OUT[0], _mybir.dt.from_np(_np.dtype(_OUT[1])), kind="ExternalOutput").ap())
    cross_attention_moe_kernel(nc, *args)
    r = _run(nc, [arrays], core_ids=[0])
    return r.results[0]["out_0"]
```

```python
import concourse.bass as bass
from concourse import mybir
from contextlib import ExitStack

F32 = mybir.dt.float32
F32R = mybir.dt.float32r
BF16 = mybir.dt.bfloat16
ALU = mybir.AluOpType
ACT = mybir.ActivationFunctionType
AX = mybir.AxisListType


def cross_attention_moe_kernel(nc, x, ctx_kv, Wq, Wkv, Wout, gate_w, gate_A, gate_B,
                               gate_up, down, gup_A, gup_B, down_A, down_B, out):
    P = 128
    B, S, H = x.shape
    L = ctx_kv.shape[2]
    HD = 16
    NH = H // HD
    E = gate_w.shape[0]
    R = gate_A.shape[0]
    I = down.shape[1]
    HC = H // P
    NT = B
    GT = 4
    NG = NT // GT
    GN = GT * P
    NC = NH // 4
    VW = HD + 1
    SLOTS_Q = (0, 0, 0, 1, 1, 2)
    SLOTS_K = (0, 1, 2, 0, 1, 0)
    NS = len(SLOTS_Q)
    KS = NS * HD
    KM = KS + 3
    SCALE = 0.25
    LORA = 2.0
    EPS = 1e-5
    MASKED = -2.0 ** 127
    ONE_ONE = 1.00193786621093750
    ORDER = (2, 3, 0, 1)
    ROUTER_AT = GT + 1
    HEAD_AT = lambda i: i % HC * (NH // HC) + i // HC
    LORA_BANK = lambda n: (5, 6, 7)[n % 3]

    ctx = ExitStack()
    with ctx:
        def sb(name, shape, dt=F32):
            return ctx.enter_context(nc.sbuf_tensor(name, shape, dt))

        def sem(name):
            return ctx.enter_context(nc.semaphore(name))

        x_sb = sb("x_sb", [P, NT, H])
        ctx_sb = sb("ctx_sb", [P, NT, 2, L])
        wq_raw = sb("wq_raw", [P, HC, H])
        wkv_raw = sb("wkv_raw", [P, 2 * HC, 2, L])
        wo_raw = sb("wo_raw", [P, HC, H])
        gw_raw = sb("gw_raw", [E, H])
        ga_raw = sb("ga_raw", [R, H])
        gb_raw = sb("gb_raw", [E, R])
        gbT = sb("gbT", [R, E])
        wqT_hi = sb("wqT_hi", [P, HC, H], F32R)
        wqT_lo = sb("wqT_lo", [P, HC, H], F32R)
        wkv_hi = sb("wkv_hi", [P, 2 * H], F32R)
        wkv_lo = sb("wkv_lo", [P, 2 * H], F32R)
        woT_hi = sb("woT_hi", [P, HC, H], F32R)
        woT_lo = sb("woT_lo", [P, HC, H], F32R)
        wr_hi = sb("wr_hi", [P, HC, P], F32R)
        wr_lo = sb("wr_lo", [P, HC, P], F32R)
        upA_raw = sb("upA_raw", [P, H])
        upB_raw = sb("upB_raw", [P, HC, E, R])
        dnA_raw = sb("dnA_raw", [P, I])
        dnB_raw = sb("dnB_raw", [P, HC, E, R])
        loraBT = sb("loraBT", [P, 2, H])
        expert_rows = sb("expert_rows", [P, E])
        up_w = sb("up_w", [P, HC, E, 2 * I])
        dn_w = sb("dn_w", [P, E, H])
        ffn_buf = up_w[:, :, :, :].rearrange("p a e n -> p (a e n)")
        silu = ffn_buf[:, 0:2 * GN].rearrange("p (k n) -> p k n", k=2)
        gated = ffn_buf[:, 2 * GN:4 * GN].rearrange("p (k n) -> p k n", k=2)
        h_f = ffn_buf[:, 4 * GN:6 * GN].rearrange("p (k n) -> p k n", k=2)
        up_hi = sb("up_hi", [P, HC, E, 2 * I], F32R)
        dn_hi = sb("dn_hi", [P, E, H], F32R)
        arena = sb("arena", [P, 2, NH, P])
        upA_bd = arena[:, 0, :, :].rearrange("p h n -> p (h n)").rearrange("p (e n) -> p e n", e=E)
        dnA_bd = arena[:, 1, 0:E, :]
        probsT = arena
        q_st = sb("q_st", [KM, 3, NH, P], BF16)
        k_st = sb("k_st", [KM, 3, NH, P], BF16)
        v_sb = sb("v_sb", [P, NT, NH, VW])
        xT_hi = sb("xT_hi", [P, HC, NT * P], F32R)
        xT_lo = sb("xT_lo", [P, HC, NT * P], F32R)
        ident = sb("ident", [P, P])
        ident_b = sb("ident_b", [P, P], BF16)
        causal = sb("causal", [P, 4, P], BF16)
        stats = sb("stats", [P, 2, NT, 6])
        mv = sb("mv", [P, 2, NT, 2])
        rstd = sb("rstd", [P, 2, NT])
        var_eps = sb("var_eps", [P, NT])
        minus_half = sb("minus_half", [P, NT])
        m_sb = sb("m_sb", [P, 2, NH])
        m_rest = sb("m_rest", [P, NH])
        m_parts = sb("m_parts", [P, 3, NH], BF16)
        mT = sb("mT", [3 * NH, P], BF16)
        oT_sb = sb("oT_sb", [P, 4, P])
        r_den = sb("r_den", [P, NH])
        o_nat = sb("o_nat", [P, NH, HD])
        oT_hi = sb("oT_hi", [P, HC, P], F32R)
        oT_lo = sb("oT_lo", [P, HC, P], F32R)
        x2hat = sb("x2hat", [P, H])
        lgT = sb("lgT", [E, GN])
        lg = sb("lg", [P, GT, E])
        lmax = sb("lmax", [P, GT])
        above = sb("above", [P, GT, E, E])
        equal = sb("equal", [P, GT, E, E])
        earlier = sb("earlier", [P, E, E])
        rank = sb("rank", [P, GT, E])
        chosen = sb("chosen", [P, GT, E])
        lsub = sb("lsub", [P, GT, E])
        lexp = sb("lexp", [P, GT, E])
        lpick = sb("lpick", [P, GT, E])
        lsum = sb("lsum", [P, GT])
        linv = sb("linv", [P, GT])
        wts = sb("wts", [P, GT, E])
        w_rest = sb("w_rest", [P, GT, E])
        w_parts = sb("w_parts", [P, GT, 3, E], BF16)
        wT = sb("wT", [3 * E, NG, GN], BF16)
        pick = sb("pick", [3 * E, E, P], BF16)
        h_hi = sb("h_hi", [P, 2, GN], F32R)
        h_lo = sb("h_lo", [P, 2, GN], F32R)

        with ExitStack() as early:
            def sbe(name, shape, dt=F32):
                return early.enter_context(nc.sbuf_tensor(name, shape, dt))
            parts = sbe("parts", [P, 4, 3, GN], BF16)
            rest = sbe("rest", [P, 4, GN])
            xhat = sbe("xhat", [P, GT, H])
            cT = sbe("cT", [P, GN], F32R)
            cT_tmp = sbe("cT_tmp", [P, GN], F32R)
        up_lo = sb("up_lo", [P, HC, E, 2 * I], F32R)
        dn_lo = sb("dn_lo", [P, E, H], F32R)

        qk_dram = nc.dram_tensor("qk_parts", (2, NT, 3, HD, NH // HC, HC, P), BF16, kind="Internal").ap()

        bank = [ctx.enter_context(nc.psum_tensor(f"bank{i}", [P, 512], F32)) for i in range(8)]

        QK_BANK = lambda j: bank[(5, 6, 7, 2)[j]]

        ld = {n: sem("ld_" + n) for n in ("x0", "x1", "ctx", "wq", "wkv", "wo", "gate", "upA", "upB",
                                          "dnA", "dnB", "up", "dn")}
        stack_loaded = [sem(f"stack_loaded{i}") for i in range(3)]
        m_loaded = [sem(f"m_loaded{i}") for i in range(2)]
        made = {}

        def S_(name):
            if name not in made:
                made[name] = sem(name)
            return made[name]

        lgT_rows = lgT
        xT_src = lambda g: slice(g * GN, (g + 1) * GN)
        ctx_v = ctx_kv.rearrange("b s l -> s b l")
        x_v = x.rearrange("b s h -> s b h")
        out_v = out.rearrange("b s h -> s b h")
        wkv_v = Wkv.rearrange("(c p) l -> p c l", p=P)

        block = ctx.enter_context(nc.Block())

        @block.sync
        def _(sp):
            for g in range(NG):
                if g == 0:
                    sp.dma_start(x_sb[:, 0:GT, :], x_v[:, 0:GT, :]).then_inc(ld["x0"], 16)
                    for k in range(2):
                        sp.dma_start(wkv_raw[:, :, k, :], wkv_v).then_inc(ld["wkv"], 16)
                    for k in range(2):
                        sp.dma_start(ctx_sb[:, :, k, :], ctx_v).then_inc(ld["ctx"], 16)
                    sp.dma_start(wq_raw[:, :, :], Wq.rearrange("(c p) h -> p c h", p=P)).then_inc(ld["wq"], 16)
                else:
                    sp.dma_start(x_sb[:, GT:NT, :], x_v[:, GT:NT, :]).then_inc(ld["x1"], 16)
            sp.dma_start(upA_raw[:, :], gup_A.rearrange("e r h -> (e r) h")).then_inc(ld["upA"], 16)
            sp.dma_start(dnA_raw[:, :], down_A.rearrange("e r i -> (e r) i")).then_inc(ld["dnA"], 16)
            for c in range(HC):
                sp.dma_start(upB_raw[:, c, :, :], gup_B.rearrange("e (c p) r -> c p e r", p=P)[c]).then_inc(ld["upB"], 16)
            for c in range(HC):
                sp.dma_start(dnB_raw[:, c, :, :], down_B.rearrange("e (c p) r -> c p e r", p=P)[c]).then_inc(ld["dnB"], 16)
            sp.dma_start(wo_raw[:, :, :], Wout.rearrange("(c p) h -> p c h", p=P)).then_inc(ld["wo"], 16)
            sp.dma_start(gw_raw[:, :], gate_w).then_inc(ld["gate"], 16)
            sp.dma_start(ga_raw[:, :], gate_A).then_inc(ld["gate"], 16)
            sp.dma_start(gb_raw[:, :], gate_B).then_inc(ld["gate"], 16)
            for c in range(HC):
                sp.dma_start(up_w[:, c, :, :], gate_up.rearrange("e (c p) o -> c p e o", p=P)[c]).then_inc(ld["up"], 16)
            sp.dma_start(dn_w[:, :, :], down.rearrange("e i h -> i e h")).then_inc(ld["dn"], 16)

            def write_parts(g, j):
                sp.wait_ge(S_("part3"), 4 * g + ORDER.index(j) + 1)
                which, c = divmod(j, HC)
                for t in range(3):
                    dst = qk_dram[which, g * GT:(g + 1) * GT, t, :, :, c].rearrange("t d h n -> (d h) t n")
                    sp.dma_start(dst, parts[:, j, t, :].rearrange("p (t n) -> p t n", t=GT)).then_inc(S_("parts_written"), 16)

            def load_stack(b):
                sp.wait_ge(S_("parts_written"), 16 * 12 * (b // GT + 1))
                if b >= 3:
                    sp.wait_ge(S_("sT_ready"), NC * (b - 2))
                for part, (first, count) in enumerate(((0, 3), (3, 2), (5, 1))):
                    src = qk_dram[0, b, part].rearrange("d h c n -> d (h c n)")[None].to_broadcast([count, HD, NH * P])
                    dst = q_st[first * HD:(first + count) * HD, b % 3, :, :].rearrange("p h n -> p (h n)")
                    sp.dma_start(dst, src).then_inc(stack_loaded[b % 3], 16)
                for first, count in ((0, 3), (3, 2), (5, 1)):
                    src = qk_dram[1, b, 0:count].rearrange("s d h c n -> (s d) (h c n)")
                    dst = k_st[first * HD:(first + count) * HD, b % 3, :, :].rearrange("p h n -> p (h n)")
                    sp.dma_start(dst, src).then_inc(stack_loaded[b % 3], 16)

            for g in range(NG):
                for j in ORDER:
                    write_parts(g, j)
                if g == 0:
                    for b in range(3):
                        load_stack(b)
            def load_max(b):
                sp.wait_ge(S_("mT_copied"), b + 1)
                sp.dma_start(q_st[KS:KM, b % 3, :, :], mT[:, :]).then_inc(m_loaded[b % 2], 16)

            load_max(0)
            for b in range(NT):
                if b + 1 < NT:
                    load_max(b + 1)
                if b + 3 < NT:
                    load_stack(b + 3)
            for g in range(NG):
                for k in range(2):
                    sp.wait_ge(S_("out_ready"), 2 * g + k + 1)
                    t0 = g * GT + 2 * k
                    sp.dma_start(out_v[:, t0:t0 + 2, :], x_sb[:, t0:t0 + 2, :]).then_inc(S_("stored"), 16)
            sp.wait_ge(S_("stored"), 16 * 2 * NG)

        @block.gpsimd
        def _(pool):
            step = [0]

            def link(ins):
                step[0] += 1
                ins.then_inc(S_("pool_chain"), 1)
                pool.wait_ge(S_("pool_chain"), step[0])

            link(pool.memset(minus_half[:, :], -0.5))
            link(pool.memset(ident[:, :], 0.0))
            link(pool.affine_select(out=ident[:, :], in_=ident[:, :], compare_op=ALU.not_equal, fill=1.0,
                                    base=0, pattern=[[-1, P]], channel_multiplier=1))
            pool.tensor_copy(ident_b[:, :], ident[:, :]).then_inc(S_("ident_made"), 1)

            def normaliser(which, lo, hi, name, n):
                pool.wait_ge(S_(name), n)
                link(pool.tensor_scalar(var_eps[:, lo:hi], mv[:, which, lo:hi, 1], EPS, None, ALU.add))
                pool.tensor_tensor(rstd[:, which, lo:hi], var_eps[:, lo:hi], minus_half[:, lo:hi], ALU.pow)\
                    .then_inc(S_("rstd1_ready" if which == 0 else "rstd2_ready"), 1)

            pool.wait_ge(S_("ident_made"), 1)
            pool.memset(k_st[KS:KM, :, :, :].bitcast(F32), ONE_ONE).then_inc(S_("k_ones"), 1)
            pool.wait_ge(S_("k_ones"), 1)
            link(pool.memset(expert_rows[:, :], 1.0))
            link(pool.affine_select(out=expert_rows[:, :], in_=expert_rows[:, :], compare_op=ALU.is_ge, fill=0.0,
                                    base=0, pattern=[[-R, E]], channel_multiplier=1))
            link(pool.affine_select(out=expert_rows[:, :], in_=expert_rows[:, :], compare_op=ALU.is_ge, fill=0.0,
                                    base=R - 1, pattern=[[R, E]], channel_multiplier=-1))
            normaliser(0, 0, GT, "mv1_ready", GT)
            link(pool.memset(causal[:, :, :], 0.0))
            pool.affine_select(out=causal[:, :, :], in_=causal[:, :, :], compare_op=ALU.is_ge, fill=MASKED,
                               base=0, pattern=[[0, 4], [-1, P]], channel_multiplier=1).then_inc(S_("causal_made"), 1)
            normaliser(0, GT, NT, "mv1_ready", NT)
            pool.memset(v_sb[:, :, :, HD:VW], 1.0).then_inc(S_("v_ones"), 1)

            def third_parts(g):
                for i, j in enumerate(ORDER):
                    pool.wait_ge(S_("part2"), 4 * g + i + 1)
                    if g:
                        pool.wait_ge(S_("parts_written"), 16 * 12 * g)
                    pool.tensor_tensor(parts[:, j, 2, :], rest[:, i, :], parts[:, j, 1, :], ALU.subtract)\
                        .then_inc(S_("part3"), 1)

            third_parts(0)
            pool.wait_ge(ld["upA"], 16)
            pool.tensor_tensor(upA_bd, upA_raw[:, None, :].to_broadcast([P, E, H]),
                               expert_rows[:, :, None].to_broadcast([P, E, H]), ALU.mult).then_inc(S_("upA_spread"), 1)
            pool.wait_ge(ld["dnA"], 16)
            pool.tensor_tensor(dnA_bd, dnA_raw[:, None, :].to_broadcast([P, E, I]),
                               expert_rows[:, :, None].to_broadcast([P, E, I]), ALU.mult).then_inc(S_("dnA_spread"), 1)
            third_parts(1)
            link(pool.memset(pick[:, :, :], 0.0))
            for t in range(3):
                link(pool.affine_select(out=pick[:, :, :], in_=pick[:, :, :], compare_op=ALU.not_equal, fill=1.0,
                                        base=-E * t, pattern=[[-1, E], [0, P]], channel_multiplier=1))
            link(pool.memset(earlier[:, :, :], 1.0))
            pool.affine_select(out=earlier[:, :, :], in_=earlier[:, :, :], compare_op=ALU.is_ge, fill=0.0,
                               base=-1, pattern=[[1, E], [-1, E]], channel_multiplier=0).then_inc(S_("router_consts"), 1)
            pool.wait_ge(S_("router_consts"), 1)

            pool.wait_ge(S_("parts_written"), 16 * 12 * NG)
            pool.wait_ge(S_("part3"), 4 * NG)
            pool.wait_ge(S_("v_proj"), 2 * NG)
            pool.wait_ge(S_("q_proj"), 2 * NG)

            for n in range(4):
                c, e0 = n // 2, (n % 2) * 4
                pool.wait_ge(S_("up_hi_ready"), n + 1)
                pool.tensor_tensor(up_lo[:, c, e0:e0 + 4, :], up_w[:, c, e0:e0 + 4, :],
                                   up_hi[:, c, e0:e0 + 4, :].bitcast(F32), ALU.subtract).then_inc(S_("lows_ready"), 1)
            for n in range(2):
                e0 = 4 * n
                pool.wait_ge(S_("dn_hi_ready"), n + 1)
                pool.tensor_tensor(dn_lo[:, e0:e0 + 4, :], dn_w[:, e0:e0 + 4, :],
                                   dn_hi[:, e0:e0 + 4, :].bitcast(F32), ALU.subtract).then_inc(S_("lows_ready"), 1)

            for b in range(NT + 2):
                if b >= 2:
                    normaliser(1, b - 2, b - 1, "mv2_ready", b - 1)
                if b < NT:
                    for c in range(NC):
                        pool.wait_ge(S_("exp_done"), NC * b + c + 1)
                        ch = probsT[:, b % 2, 4 * c:4 * c + 4, :]
                        pool.affine_select(out=ch, in_=ch, compare_op=ALU.is_ge, fill=0.0, base=0,
                                           pattern=[[0, 4], [1, P]], channel_multiplier=-1).then_inc(S_("probs_ready"), 1)

        @block.scalar
        def _(act):
            def high(out_, in_, done, scale=1.0):
                act.activation(out_, in_, ACT.Copy, scale=scale).then_inc(S_(done), 1)

            act.wait_ge(S_("wkv_T"), 1)
            high(wkv_hi[:, 0:H].rearrange("p (a d h) -> p a h d", a=HC, d=HD),
                 bank[3][:, 0:H].rearrange("p (a h d) -> p a h d", a=HC, d=HD), "wkv_hi_ready")
            high(wkv_hi[:, H:2 * H], bank[3][:, H:2 * H], "wkv_hi_ready")
            act.wait_ge(S_("wq_T"), 1)
            for ic in range(HC):
                high(wqT_hi[:, ic, :].rearrange("p (a d h) -> p a h d", a=HC, d=HD),
                     bank[2][:, ic * H:(ic + 1) * H].rearrange("p (a h d) -> p a h d", a=HC, d=HD), "wq_hi_ready", SCALE)
            for g in range(NG):
                act.wait_ge(S_("c_T"), g + 1)
                if g:
                    act.wait_ge(S_("v_proj"), 2 * g)
                    act.wait_ge(S_("cT_lo"), g)
                high(cT[0:L, :], bank[4][0:L, :], "cT_hi")
                high(cT_tmp[L:P, :], bank[4][L:P, :], "cT_hi")
                for ic in range(HC):
                    act.wait_ge(S_("x_T"), HC * g + ic + 1)
                    high(xT_hi[:, ic, xT_src(g)], bank[ic][:, :], "xT_hi_ready")
                for k in range(2):
                    act.wait_ge(S_("v_proj"), 2 * g + k + 1)
                    t0 = g * GT + 2 * k
                    high(v_sb[:, t0:t0 + 2, :, 0:HD],
                         bank[3 + k][:, :].rearrange("p (t h d) -> p t h d", t=2, d=HD), "v_ready")
                for i, j in enumerate(ORDER):
                    act.wait_ge(S_("q_proj" if j < HC else "k_proj"), HC * g + j % HC + 1)
                    if g:
                        act.wait_ge(S_("parts_written"), 16 * 12 * g)
                    high(parts[:, j, 0, :], QK_BANK(j)[:, :], "part1")
                    if i:
                        act.wait_ge(S_("rest_ready"), 4 * g + i)
                        high(parts[:, ORDER[i - 1], 1, :], rest[:, i - 1, :], "part2")
                act.wait_ge(S_("rest_ready"), 4 * g + 4)
                high(parts[:, ORDER[3], 1, :], rest[:, 3, :], "part2")
            act.wait_ge(S_("lora_T"), 1)
            high(loraBT[:, :, :].rearrange("p a n -> p (a n)"), bank[1][:, :], "lora_ready", LORA)
            act.wait_ge(S_("gb_T"), 1)
            high(gbT[:, :], bank[2][0:R, 0:E], "gbT_ready", LORA)
            act.wait_ge(S_("wo_T"), 1)
            high(woT_hi[:, :, :].rearrange("p a n -> p (a n)"), bank[0][:, :], "wo_hi_ready")
            act.wait_ge(S_("wr_T"), 1)
            act.wait_ge(S_("wr_zero"), 2)
            high(wr_hi[:, :, 0:E], bank[3][:, 0:HC * E].rearrange("p (a e) -> p a e", a=HC), "wr_hi_ready")
            for n in range(4):
                c, e0 = n // 2, (n % 2) * 4
                act.wait_ge(S_("up_merged"), (n + 1) * 2)
                high(up_hi[:, c, e0:e0 + 4, :], up_w[:, c, e0:e0 + 4, :], "up_hi_ready")
            for n in range(2):
                act.wait_ge(S_("dn_merged"), (n + 1) * 2)
                high(dn_hi[:, 4 * n:4 * n + 4, :], dn_w[:, 4 * n:4 * n + 4, :], "dn_hi_ready")

            def copy_logits(g, bk):
                act.wait_ge(S_("lgT_ready"), g + 1)
                high(lgT[:, :], bk[0:E, :], "lgT_copied")

            def exp_logits(g):
                act.wait_ge(S_("lsub_ready"), g + 1)
                act.activation(lexp[:, :, :], lsub[:, :, :], ACT.Exp).then_inc(S_("lexp_ready"), 1)

            def copy_weights(g):
                act.wait_ge(S_("wT_ready"), g + 1)
                act.activation(wT[:, g, :], bank[5][0:3 * E, 0:GN // 2].bitcast(BF16), ACT.Copy).then_inc(S_("wT_copied"), 1)

            def mT_copy(b):
                act.wait_ge(S_("mT_ready"), b + 1)
                if b:
                    act.wait_ge(m_loaded[(b - 1) % 2], 16 * ((b - 1) // 2 + 1))
                act.activation(mT[:, :], bank[5][0:3 * NH, 0:P // 2].bitcast(BF16), ACT.Copy).then_inc(S_("mT_copied"), 1)

            def exp_chunk(b, c):
                act.wait_ge(S_("sT_ready"), NC * b + c + 1)
                if b >= 2 and c == 0:
                    act.wait_ge(S_("pv_done"), b - 1)
                if b == 0 and c == 0:
                    act.wait_ge(S_("up_lora"), HC * E // 2)
                    act.wait_ge(S_("dn_lora"), E // 2)
                act.activation(probsT[:, b % 2, 4 * c:4 * c + 4, :].rearrange("p h n -> p (h n)"),
                               bank[2 + c % 2][:, :], ACT.Exp).then_inc(S_("exp_done"), 1)

            def silu_step(n):
                act.wait_ge(S_("gate_ready"), n + 1)
                if n >= 2:
                    act.wait_ge(S_("gated_ready"), n - 1)
                act.activation(silu[:, n % 2, :], bank[n % 2][:, :], ACT.Silu).then_inc(S_("silu_ready"), 1)

            mT_copy(0)
            for b in range(NT + 2):
                if b < NT:
                    exp_chunk(b, 0)
                    exp_chunk(b, 1)
                if b >= 2:
                    act.wait_ge(S_("x2_T"), b - 1)
                    high(xT_hi[:, :, (b - 2) * P:(b - 1) * P],
                         bank[7][:, HC * P:2 * HC * P].rearrange("p (a n) -> p a n", a=HC), "x2T_hi")
                if b < NT:
                    exp_chunk(b, 2)
                    exp_chunk(b, 3)
                if 1 <= b <= NT:
                    act.wait_ge(S_("o_T"), b)
                    if b >= 2:
                        act.wait_ge(S_("o_out"), b - 1)
                    high(oT_hi[:, :, :].rearrange("p a n -> p (a n)"), bank[6][:, 0:HC * P], "oT_hi_ready")
                if b == NT:
                    act.wait_ge(S_("lows_ready"), 6)
                    silu_step(0)
                if b < NT:
                    if b + 1 < NT:
                        mT_copy(b + 1)
                    act.wait_ge(S_("pv_done"), b + 1)
                    if b:
                        act.wait_ge(S_("on_ready"), b)
                    high(oT_sb[:, :, :].rearrange("p a n -> p (a n)"), bank[4][:, :], "oT_copied")
                if b == ROUTER_AT:
                    copy_logits(0, bank[6])
                if b == ROUTER_AT + 1:
                    exp_logits(0)
                if b == ROUTER_AT + 2:
                    copy_weights(0)

            for n in range(NG * E):
                k = n % 2
                act.wait_ge(S_("h_ready"), n + 1)
                if n >= 2:
                    act.wait_ge(S_("down_done"), n - 1)
                high(h_hi[:, k, :], h_f[:, k, :], "h_hi_ready")
                if n + 1 < NG * E:
                    silu_step(n + 1)
                if n == 1:
                    copy_logits(1, bank[5])
                if n == 2:
                    exp_logits(1)
                if n == 4:
                    copy_weights(1)

        @block.vector
        def _(dve):
            step = [0]

            def link(ins):
                step[0] += 1
                ins.then_inc(S_("dve_chain"), 1)
                dve.wait_ge(S_("dve_chain"), step[0])

            def low(out_, in_, hi, done, scale=1.0):
                dve.scalar_tensor_tensor(out=out_, in0=in_, scalar=scale, in1=hi.bitcast(F32), op0=ALU.mult,
                                         op1=ALU.subtract).then_inc(S_(done), 1)

            def norm_stats(which, t, done, src=None):
                link(dve.bn_stats(stats[:, which, t, :], x_sb[:, t, :]))
                dve.bn_aggr(mv[:, which, t, :], stats[:, which, t, :]).then_inc(S_(done), 1)

            def normalise(which, t, out_, done):
                dve.tensor_scalar(out_, x_sb[:, t, :], mv[:, which, t, 0:1], rstd[:, which, t:t + 1],
                                  ALU.subtract, ALU.mult).then_inc(S_(done), 1)

            dve.memset(wkv_lo[L:P, :].bitcast(F32), 0.0).then_inc(S_("wkv_zero"), 1)
            dve.memset(wr_hi[:, :, :].bitcast(F32), 0.0).then_inc(S_("wr_zero"), 1)
            dve.memset(wr_lo[:, :, :].bitcast(F32), 0.0).then_inc(S_("wr_zero"), 1)
            for g in range(NG):
                if g == 0:
                    dve.wait_ge(ld["x0"], 16)
                    for t in range(GT):
                        norm_stats(0, t, "mv1_ready")
                    dve.wait_ge(S_("wkv_hi_ready"), 2)
                    for a in range(HC):
                        cols = slice(a * P, (a + 1) * P)
                        low(wkv_lo[0:L, cols].rearrange("p (d h) -> p h d", d=HD),
                            bank[3][0:L, cols].rearrange("p (h d) -> p h d", d=HD),
                            wkv_hi[0:L, cols].rearrange("p (d h) -> p h d", d=HD), "wkv_lo_ready")
                    low(wkv_lo[0:L, H:2 * H], bank[3][0:L, H:2 * H], wkv_hi[0:L, H:2 * H], "wkv_lo_ready")
                dve.wait_ge(S_("rstd1_ready"), g + 1)
                if g:
                    dve.wait_ge(S_("x_T"), HC * g)
                for t in range(GT):
                    normalise(0, g * GT + t, xhat[:, t, :], "xhat_ready")
                if g + 1 < NG:
                    dve.wait_ge(ld["x1"], 16)
                    for t in range((g + 1) * GT, (g + 2) * GT):
                        norm_stats(0, t, "mv1_ready")
                if g == 0:
                    dve.wait_ge(S_("wq_hi_ready"), 2)
                    for ic in range(HC):
                        for a in range(HC):
                            cols = slice(a * P, (a + 1) * P)
                            low(wqT_lo[:, ic, cols].rearrange("p (d h) -> p h d", d=HD),
                                bank[2][:, ic * H + a * P:ic * H + (a + 1) * P].rearrange("p (h d) -> p h d", d=HD),
                                wqT_hi[:, ic, cols].rearrange("p (d h) -> p h d", d=HD), "wq_lo_ready", SCALE)
                dve.wait_ge(S_("cT_hi"), 2 * (g + 1))
                low(cT[L:P, :], bank[4][L:P, :], cT_tmp[L:P, :], "cT_lo")
                for ic in range(HC):
                    dve.wait_ge(S_("xT_hi_ready"), HC * g + ic + 1)
                    low(xT_lo[:, ic, xT_src(g)], bank[ic][:, :], xT_hi[:, ic, xT_src(g)], "xT_lo_ready")
                for i, j in enumerate(ORDER):
                    dve.wait_ge(S_("part1"), 4 * g + i + 1)
                    if g:
                        dve.wait_ge(S_("part3"), 4 * (g - 1) + i + 1)
                    dve.tensor_tensor(rest[:, i, :], QK_BANK(j)[:, :], parts[:, j, 0, :], ALU.subtract)\
                        .then_inc(S_("rest_ready"), 1)
            dve.wait_ge(S_("wo_hi_ready"), 1)
            low(woT_lo[:, :, :].rearrange("p a n -> p (a n)"), bank[0][:, :],
                woT_hi[:, :, :].rearrange("p a n -> p (a n)"), "wo_lo_ready")
            dve.wait_ge(S_("wr_hi_ready"), 1)
            low(wr_lo[:, :, 0:E], bank[3][:, 0:HC * E].rearrange("p (a e) -> p a e", a=HC), wr_hi[:, :, 0:E], "wr_lo_ready")
            dve.wait_ge(S_("o_bank_free"), 1)
            dve.memset(bank[4][:, :], 0.0).then_inc(S_("o_zero"), 1)
            dve.wait_ge(ld["up"], 32)
            for n in range(HC * E // 2):
                c, e0 = divmod(2 * n, E)
                dve.wait_ge(S_("up_lora"), n + 1)
                dve.tensor_tensor(up_w[:, c, e0:e0 + 2, :], bank[LORA_BANK(n)][:, :].rearrange("p (e n) -> p e n", e=2),
                                  up_w[:, c, e0:e0 + 2, :], ALU.add).then_inc(S_("up_merged"), 1)
            dve.wait_ge(ld["dn"], 16)
            for n in range(E // 2):
                dve.wait_ge(S_("dn_lora"), n + 1)
                dve.tensor_tensor(dn_w[:, 2 * n:2 * n + 2, :], bank[LORA_BANK(n)][:, :].rearrange("p (e n) -> p e n", e=2),
                                  dn_w[:, 2 * n:2 * n + 2, :], ALU.add).then_inc(S_("dn_merged"), 1)

            def max_chunk(b, c):
                dve.wait_ge(S_("s_ready"), NC * b + c + 1)
                dve.reduce_max(m_sb[:, b % 2, 4 * c:4 * c + 4], bank[c % 2][:, :].rearrange("p (h n) -> p h n", h=4), AX.X)\
                    .then_inc(S_("max_done"), 1)

            def max_parts(b):
                m = m_sb[:, b % 2, :]
                dve.wait_ge(S_("max_done"), NC * (b + 1))
                if b:
                    dve.wait_ge(S_("mT_ready"), b)
                link(dve.tensor_scalar(m_parts[:, 0, :], m, -1.0, None, ALU.mult))
                link(dve.scalar_tensor_tensor(out=m_rest[:, :], in0=m, scalar=-1.0, in1=m_parts[:, 0, :],
                                              op0=ALU.mult, op1=ALU.subtract))
                link(dve.tensor_copy(m_parts[:, 1, :], m_rest[:, :]))
                dve.tensor_tensor(m_parts[:, 2, :], m_rest[:, :], m_parts[:, 1, :], ALU.subtract)\
                    .then_inc(S_("m_parts_ready"), 1)

            def route_choose(g):
                dve.wait_ge(S_("lg_ready"), g + 1)
                link(dve.tensor_copy(lg[:, :, :], bank[5][:, 0:GT * E].rearrange("p (t e) -> p t e", e=E)))
                link(dve.reduce_max(lmax[:, :], lg[:, :, :], AX.X))
                dve.tensor_tensor(lsub[:, :, :], lg[:, :, :], lmax[:, :, None].to_broadcast([P, GT, E]), ALU.subtract)\
                    .then_inc(S_("lsub_ready"), 1)
                other = lg[:, :, None, :].to_broadcast([P, GT, E, E])
                mine = lg[:, :, :, None].to_broadcast([P, GT, E, E])
                link(dve.tensor_tensor(above[:, :, :, :], other, mine, ALU.is_gt))
                link(dve.tensor_tensor(equal[:, :, :, :], other, mine, ALU.is_equal))
                link(dve.tensor_tensor(equal[:, :, :, :], equal[:, :, :, :],
                                       earlier[:, None, :, :].to_broadcast([P, GT, E, E]), ALU.mult))
                link(dve.tensor_tensor(above[:, :, :, :], above[:, :, :, :], equal[:, :, :, :], ALU.add))
                link(dve.reduce_sum(rank[:, :, :], above[:, :, :, :], AX.X))
                link(dve.tensor_scalar(chosen[:, :, :], rank[:, :, :], 1.5, None, ALU.is_lt))

            def route_weights(g):
                dve.wait_ge(S_("lexp_ready"), g + 1)
                link(dve.tensor_tensor(lpick[:, :, :], lexp[:, :, :], chosen[:, :, :], ALU.mult))
                link(dve.reduce_sum(lsum[:, :], lpick[:, :, :], AX.X))
                link(dve.reciprocal(linv[:, :], lsum[:, :]))
                link(dve.tensor_tensor(wts[:, :, :], lpick[:, :, :], linv[:, :, None].to_broadcast([P, GT, E]), ALU.mult))
                link(dve.tensor_copy(w_parts[:, :, 0, :], wts[:, :, :]))
                link(dve.tensor_tensor(w_rest[:, :, :], wts[:, :, :], w_parts[:, :, 0, :], ALU.subtract))
                link(dve.tensor_copy(w_parts[:, :, 1, :], w_rest[:, :, :]))
                dve.tensor_tensor(w_parts[:, :, 2, :], w_rest[:, :, :], w_parts[:, :, 1, :], ALU.subtract)\
                    .then_inc(S_("w_parts_ready"), 1)

            def gate_and_weigh(n):
                k = n % 2
                if n == 0:
                    dve.wait_ge(S_("lows_ready"), 6)
                dve.wait_ge(S_("silu_ready"), n + 1)
                dve.wait_ge(S_("up_ready"), n + 1)
                dve.tensor_tensor(gated[:, k, :], bank[2 + k][:, :], silu[:, k, :], ALU.mult).then_inc(S_("gated_ready"), 1)
                dve.wait_ge(S_("gated_ready"), n + 1)
                dve.wait_ge(S_("weight_ready"), n + 1)
                dve.tensor_tensor(h_f[:, k, :], bank[4][:, :], gated[:, k, :], ALU.mult).then_inc(S_("h_ready"), 1)

            for c in range(NC):
                max_chunk(0, c)
            max_parts(0)
            max_chunk(1, 0)
            max_chunk(1, 1)
            dve.wait_ge(S_("router_consts"), 1)
            for b in range(NT + 2):
                if b + 1 < NT:
                    max_chunk(b + 1, 2)
                if b >= 2:
                    dve.wait_ge(S_("rstd2_ready"), b - 1)
                    if b >= 3:
                        dve.wait_ge(S_("x2_T"), b - 2)
                    normalise(1, b - 2, x2hat[:, :], "x2hat_ready")
                if 1 <= b <= NT:
                    dve.wait_ge(S_("on_ready"), b)
                    on = bank[5][:, :].rearrange("p (h w) -> p h w", h=NH)
                    link(dve.reciprocal(r_den[:, :], on[:, :, HD]))
                    dve.tensor_tensor(o_nat[:, :, :], on[:, :, 0:HD], r_den[:, :, None].to_broadcast([P, NH, HD]), ALU.mult)\
                        .then_inc(S_("o_nat_ready"), 1)
                if b + 1 < NT:
                    max_chunk(b + 1, 3)
                    max_parts(b + 1)
                if b == NT + 1:
                    gate_and_weigh(0)
                if b >= 2:
                    dve.wait_ge(S_("x2T_hi"), b - 1)
                    low(xT_lo[:, :, (b - 2) * P:(b - 1) * P],
                        bank[7][:, HC * P:2 * HC * P].rearrange("p (a n) -> p a n", a=HC),
                        xT_hi[:, :, (b - 2) * P:(b - 1) * P], "x2T_lo")
                if 1 <= b <= NT:
                    dve.wait_ge(S_("oT_hi_ready"), b)
                    low(oT_lo[:, :, :].rearrange("p a n -> p (a n)"), bank[6][:, 0:HC * P],
                        oT_hi[:, :, :].rearrange("p a n -> p (a n)"), "oT_lo_ready")
                if b + 2 < NT:
                    max_chunk(b + 2, 0)
                if 1 <= b <= NT:
                    t = b - 1
                    dve.wait_ge(S_("o_out"), b)
                    link(dve.tensor_tensor(x_sb[:, t, :], bank[7][:, 0:H], x_sb[:, t, :], ALU.add))
                    norm_stats(1, t, "mv2_ready")
                if b + 2 < NT:
                    max_chunk(b + 2, 1)
                if b == ROUTER_AT + 1:
                    route_choose(0)
                    route_weights(0)

            for n in range(NG * E):
                g, e = divmod(n, E)
                k = n % 2
                if n:
                    gate_and_weigh(n)
                dve.wait_ge(S_("h_hi_ready"), n + 1)
                dve.tensor_tensor(h_lo[:, k, :], h_f[:, k, :], h_hi[:, k, :].bitcast(F32), ALU.subtract)\
                    .then_inc(S_("h_lo_ready"), 1)
                if n == 2:
                    route_choose(1)
                if n == 3:
                    route_weights(1)
                if e == E - 1:
                    dve.wait_ge(S_("down_done"), n + 1)
                    for k2 in range(2):
                        t0 = g * GT + 2 * k2
                        dve.tensor_tensor(x_sb[:, t0:t0 + 2, :], bank[6 + k2][:, :].rearrange("p (t n) -> p t n", t=2),
                                          x_sb[:, t0:t0 + 2, :], ALU.add).then_inc(S_("out_ready"), 1)

        @block.tensor
        def _(pe):
            def products(out_, pairs, done=None, start=True, stop=True, **kw):
                for i, (a, m) in enumerate(pairs):
                    last = pe.matmul(out_, a, m, start=start and i == 0, stop=stop and i == len(pairs) - 1, **kw)
                if done:
                    last.then_inc(S_(done), 1)

            pe.wait_ge(S_("ident_made"), 1)
            pe.wait_ge(ld["wkv"], 32)
            for oc in range(4):
                last = pe.transpose(bank[3][:, oc * P:(oc + 1) * P], wkv_raw[:, oc, :, :].rearrange("p k l -> p (k l)"), ident[:, :])
            last.then_inc(S_("wkv_T"), 1)

            def context_T(g):
                if g == 0:
                    pe.wait_ge(ld["ctx"], 32)
                else:
                    pe.wait_ge(S_("v_ready"), 2 * g)
                for t in range(GT):
                    last = pe.transpose(bank[4][:, t * P:(t + 1) * P],
                                        ctx_sb[:, g * GT + t, :, :].rearrange("p k l -> p (k l)"), ident[:, :])
                last.then_inc(S_("c_T"), 1)

            def x_T(g):
                pe.wait_ge(S_("xhat_ready"), GT * (g + 1))
                if g:
                    pe.wait_ge(S_("xT_lo_ready"), HC * g)
                for ic in range(HC):
                    for t in range(GT):
                        last = pe.transpose(bank[ic][:, t * P:(t + 1) * P], xhat[:, t, ic * P:(ic + 1) * P], ident[:, :])
                    last.then_inc(S_("x_T"), 1)

            def kv_proj(g):
                pe.wait_ge(S_("wkv_lo_ready"), HC + 1)
                pe.wait_ge(S_("wkv_zero"), 1)
                pe.wait_ge(S_("wkv_hi_ready"), 2)
                pe.wait_ge(S_("wq_lo_ready"), HC * HC)
                pe.wait_ge(S_("cT_lo"), g + 1)
                if g:
                    pe.wait_ge(S_("rest_ready"), 4 * g)
                    pe.wait_ge(S_("v_ready"), 2 * g)
                for oc in range(HC):
                    cols = slice(oc * P, (oc + 1) * P)
                    products(QK_BANK(HC + oc)[:, :], [(wkv_hi[:, cols], cT[:, :]), (wkv_lo[:, cols], cT[:, :])], "k_proj")
                for k in range(2):
                    for t in range(2):
                        tok = slice((2 * k + t) * P, (2 * k + t + 1) * P)
                        products(bank[3 + k][:, t * H:(t + 1) * H],
                                 [(cT[:, tok], wkv_hi[:, H:2 * H]), (cT[:, tok], wkv_lo[:, H:2 * H])],
                                 "v_proj" if t else None)

            def q_proj(g):
                pe.wait_ge(S_("xT_lo_ready"), HC * (g + 1))
                for oc in range(HC):
                    cols = slice(oc * P, (oc + 1) * P)
                    products(QK_BANK(oc)[:, :],
                             [(w[:, ic, cols], xt[:, ic, xT_src(g)]) for ic in range(HC)
                              for w, xt in ((wqT_hi, xT_hi), (wqT_hi, xT_lo), (wqT_lo, xT_hi))], "q_proj")

            pe.wait_ge(ld["wq"], 16)
            for ic in range(HC):
                for oc in range(HC):
                    last = pe.transpose(bank[2][:, ic * H + oc * P:ic * H + (oc + 1) * P],
                                        wq_raw[:, oc, ic * P:(ic + 1) * P], ident[:, :])
            last.then_inc(S_("wq_T"), 1)
            for g in range(NG):
                context_T(g)
                x_T(g)
                kv_proj(g)
                q_proj(g)

            pe.wait_ge(ld["upB"], 32)
            pe.wait_ge(ld["dnB"], 32)
            pe.wait_ge(S_("xT_lo_ready"), HC * NG)
            for k, raw in enumerate((upB_raw, dnB_raw)):
                for c in range(HC):
                    last = pe.transpose(bank[1][:, k * H + c * P:k * H + (c + 1) * P],
                                        raw[:, c, :, :].rearrange("p e r -> p (e r)"), ident[:, :])
            last.then_inc(S_("lora_T"), 1)
            pe.wait_ge(ld["gate"], 48)
            pe.wait_ge(S_("rest_ready"), 4 * NG)
            pe.transpose(bank[2][0:R, 0:E], gb_raw[:, :], ident[0:E, 0:E]).then_inc(S_("gb_T"), 1)
            pe.wait_ge(ld["wo"], 16)
            for ic in range(HC):
                for oc in range(HC):
                    last = pe.transpose(bank[0][:, ic * H + oc * P:ic * H + (oc + 1) * P],
                                        wo_raw[:, oc, ic * P:(ic + 1) * P], ident[:, :])
            last.then_inc(S_("wo_T"), 1)
            pe.wait_ge(S_("v_ready"), 2 * NG)
            pe.wait_ge(S_("gbT_ready"), 1)
            for ic in range(HC):
                products(bank[3][:, ic * E:(ic + 1) * E],
                         [(gw_raw[:, ic * P:(ic + 1) * P], ident[0:E, 0:E]), (ga_raw[:, ic * P:(ic + 1) * P], gbT[:, :])],
                         "wr_T" if ic else None)
            pe.wait_ge(S_("lora_ready"), 1)
            pe.wait_ge(S_("upA_spread"), 1)
            pe.matmul(bank[4][0:E, 0:E], gw_raw[:, 0:E], ident[0:E, 0:E], start=True, stop=True).then_inc(S_("o_bank_free"), 1)
            for n in range(HC * E // 2):
                c, e0 = divmod(2 * n, E)
                if n >= 3:
                    pe.wait_ge(S_("up_merged"), n - 2)
                for k in range(2):
                    products(bank[LORA_BANK(n)][:, k * H:(k + 1) * H],
                             [(upA_bd[:, e0 + k, c * P:(c + 1) * P], loraBT[:, 0, :])], "up_lora" if k else None)
            pe.wait_ge(S_("dnA_spread"), 1)
            for n in range(E // 2):
                pe.wait_ge(S_("up_merged"), min(HC * E // 2, HC * E // 2 - 1 + n))
                if n >= 3:
                    pe.wait_ge(S_("dn_merged"), n - 2)
                for k in range(2):
                    products(bank[LORA_BANK(n)][:, k * H:(k + 1) * H],
                             [(dnA_bd[:, 2 * n + k, :], loraBT[:, 1, :])], "dn_lora" if k else None)

            def s_chunk(b, c):
                n = NC * b + c
                if c == 0:
                    pe.wait_ge(stack_loaded[b % 3], 16 * 6 * (b // 3 + 1))
                if n >= 2:
                    pe.wait_ge(S_("max_done"), n - 1)
                pe.matmul(bank[c % 2][:, :], ident_b[:, :], causal[:, :, :].rearrange("p h n -> p (h n)"),
                          start=True, stop=True, skip_group_check=True)
                for j in range(4):
                    h = 4 * c + j
                    last = pe.matmul(bank[c % 2][:, j * P:(j + 1) * P], q_st[0:KS, b % 3, h, :], k_st[0:KS, b % 3, h, :],
                                     start=False, stop=True, skip_group_check=True)
                last.then_inc(S_("s_ready"), 1)

            def sT_chunk(b, c):
                n = NC * b + c
                if c == 0:
                    pe.wait_ge(m_loaded[b % 2], 16 * (b // 2 + 1))
                if n >= 2:
                    pe.wait_ge(S_("exp_done"), n - 1)
                for j in range(4):
                    h = 4 * c + j
                    last = pe.matmul(bank[2 + c % 2][:, j * P:(j + 1) * P], k_st[0:KM, b % 3, h, :], q_st[0:KM, b % 3, h, :],
                                     start=True, stop=True)
                last.then_inc(S_("sT_ready"), 1)

            def max_T(b):
                pe.wait_ge(S_("m_parts_ready"), b + 1)
                pe.transpose(bank[5][0:3 * NH, 0:P // 2].bitcast(BF16), m_parts[:, :, :].rearrange("p t h -> p (t h)"),
                             ident_b[:, :]).then_inc(S_("mT_ready"), 1)

            def lgT(g, bk):
                pe.wait_ge(S_("x2T_lo"), GT * (g + 1))
                products(bk[:, :], [(w[:, ic, :], xt[:, ic, xT_src(g)]) for ic in range(HC)
                                    for w, xt in ((wr_hi, xT_hi), (wr_hi, xT_lo), (wr_lo, xT_hi))], "lgT_ready")

            def lg_T(g):
                pe.wait_ge(S_("lgT_copied"), g + 1)
                for t in range(GT):
                    last = pe.transpose(bank[5][:, t * E:(t + 1) * E], lgT_rows[:, t * P:(t + 1) * P], ident[0:E, 0:E])
                last.then_inc(S_("lg_ready"), 1)

            def w_T(g):
                pe.wait_ge(S_("w_parts_ready"), g + 1)
                for t in range(GT):
                    last = pe.transpose(bank[5][0:3 * E, t * P // 2:(t + 1) * P // 2].bitcast(BF16),
                                        w_parts[:, t, :, :].rearrange("p k e -> p (k e)"), ident_b[:, :])
                last.then_inc(S_("wT_ready"), 1)

            def gate_up_half(n, half, done):
                g, e = divmod(n, E)
                cols = slice(half * I, (half + 1) * I)
                products(bank[2 * half + n % 2][:, :],
                         [(w[:, ic, e, cols], xt[:, ic, xT_src(g)]) for ic in range(HC)
                          for w, xt in ((up_hi, xT_hi), (up_hi, xT_lo), (up_lo, xT_hi))], done)

            def gate_step(n):
                if n >= 2:
                    pe.wait_ge(S_("silu_ready"), n - 1)
                gate_up_half(n, 0, "gate_ready")

            def up_step(n):
                if n >= 2:
                    pe.wait_ge(S_("gated_ready"), n - 1)
                gate_up_half(n, 1, "up_ready")

            def weight_step(n):
                g, e = divmod(n, E)
                if e == 0:
                    pe.wait_ge(S_("wT_copied"), g + 1)
                if n:
                    pe.wait_ge(S_("h_ready"), n)
                products(bank[4][:, :], [(pick[:, e, :], wT[:, g, :])], "weight_ready")

            def down_step(n):
                g, e = divmod(n, E)
                k = n % 2
                pe.wait_ge(S_("h_lo_ready"), n + 1)
                if e == 0 and g:
                    pe.wait_ge(S_("out_ready"), 2 * g)
                for t in range(GT):
                    tok = slice(t * P, (t + 1) * P)
                    for i, (a, w) in enumerate(((h_hi, dn_hi), (h_hi, dn_lo), (h_lo, dn_hi))):
                        last = pe.matmul(bank[6 + t // 2][:, (t % 2) * H:(t % 2 + 1) * H], a[:, k, tok], w[:, e, :],
                                         start=e == 0 and t % 2 == 0 and i == 0, stop=e == E - 1 and i == 2,
                                         skip_group_check=True)
                last.then_inc(S_("down_done"), 1)

            pe.wait_ge(S_("up_merged"), HC * E // 2)
            pe.wait_ge(S_("dn_merged"), E // 2)
            pe.wait_ge(S_("wo_lo_ready"), 1)
            pe.wait_ge(S_("wr_lo_ready"), 1)
            pe.wait_ge(S_("causal_made"), 1)
            pe.wait_ge(S_("k_ones"), 1)
            pe.wait_ge(S_("v_ones"), 1)
            pe.wait_ge(S_("o_zero"), 1)
            for c in range(NC):
                s_chunk(0, c)
            s_chunk(1, 0)
            max_T(0)
            s_chunk(1, 1)
            for b in range(NT + 2):
                if b + 1 < NT:
                    s_chunk(b + 1, 2)
                if b < NT:
                    sT_chunk(b, 0)
                if b < NT:
                    sT_chunk(b, 1)
                if 1 <= b <= NT:
                    pe.wait_ge(S_("oT_copied"), b)
                    if b < NT:
                        pe.wait_ge(S_("mT_copied"), b + 1)
                    if b == ROUTER_AT + 2:
                        pe.wait_ge(S_("lsub_ready"), 1)
                    if b == ROUTER_AT + 3:
                        pe.wait_ge(S_("wT_copied"), 1)
                    for c in range(4):
                        last = pe.transpose(bank[5][:, c * P:(c + 1) * P], oT_sb[:, c, :], ident[:, :])
                    last.then_inc(S_("on_ready"), 1)
                if b + 1 < NT:
                    s_chunk(b + 1, 3)
                if b == NT:
                    pe.wait_ge(S_("lows_ready"), 6)
                    pe.wait_ge(S_("exp_done"), NC * NT)
                    gate_step(0)
                if b == NT + 1:
                    up_step(1)
                if b >= 2:
                    pe.wait_ge(S_("x2hat_ready"), b - 1)
                    for ic in range(HC):
                        last = pe.transpose(bank[7][:, (HC + ic) * P:(HC + ic + 1) * P], x2hat[:, ic * P:(ic + 1) * P],
                                            ident[:, :])
                    last.then_inc(S_("x2_T"), 1)
                if b < NT:
                    sT_chunk(b, 2)
                    sT_chunk(b, 3)
                if b == NT:
                    up_step(0)
                if 1 <= b <= NT:
                    pe.wait_ge(S_("o_nat_ready"), b)
                    if b == ROUTER_AT + 1:
                        pe.wait_ge(S_("lgT_copied"), 1)
                    for ic in range(HC):
                        last = pe.transpose(bank[6][:, ic * P:(ic + 1) * P],
                                            o_nat[:, :, :].rearrange("p h d -> p (h d)")[:, ic * P:(ic + 1) * P], ident[:, :])
                    last.then_inc(S_("o_T"), 1)
                if b + 1 < NT:
                    max_T(b + 1)
                if b + 2 < NT:
                    s_chunk(b + 2, 0)
                if b == NT:
                    weight_step(0)
                    gate_step(1)
                if 1 <= b <= NT:
                    pe.wait_ge(S_("oT_lo_ready"), b)
                    if b >= 2:
                        pe.wait_ge(S_("x2T_lo"), b - 1)
                    products(bank[7][:, 0:H], [(a[:, ic, :], w[:, ic, :]) for ic in range(HC)
                                               for a, w in ((oT_hi, woT_hi), (oT_hi, woT_lo), (oT_lo, woT_hi))], "o_out")
                if b == ROUTER_AT:
                    lgT(0, bank[6])
                if b + 2 < NT:
                    s_chunk(b + 2, 1)
                if b < NT:
                    for i in range(NH):
                        if i % 4 == 0:
                            pe.wait_ge(S_("probs_ready"), NC * b + i // 4 + 1)
                        if i == 0 and b:
                            pe.wait_ge(S_("oT_copied"), b)
                        h = HEAD_AT(i)
                        c, j = divmod(h, 4)
                        last = pe.matmul(bank[4][32 * j:32 * j + VW, c * P:(c + 1) * P], v_sb[:, b, h, :],
                                         probsT[:, b % 2, i, :], start=True, stop=True)
                    last.then_inc(S_("pv_done"), 1)
                if b == ROUTER_AT + 1:
                    pe.wait_ge(S_("mT_copied"), b + 2)
                    lg_T(0)
                if b == ROUTER_AT + 2:
                    w_T(0)

            pe.wait_ge(S_("x2T_lo"), NT)
            for n in range(NG * E):
                if n >= 1 and n + 1 < NG * E:
                    gate_step(n + 1)
                    up_step(n + 1)
                down_step(n)
                if n + 1 < NG * E:
                    weight_step(n + 1)
                if n == 0:
                    lgT(1, bank[5])
                if n == 1:
                    lg_T(1)
                if n == 3:
                    w_T(1)


_INS = ["x", "ctx_512", "L0_xattn_Wq", "L0_xattn_Wkv_expand", "L0_xattn_Wout", "L0_ffn_gate_weight",
        "L0_ffn_gate_lora_A", "L0_ffn_gate_lora_B", "L0_ffn_gate_up_proj", "L0_ffn_down_proj",
        "L0_ffn_gup_lora_A", "L0_ffn_gup_lora_B", "L0_ffn_down_lora_A", "L0_ffn_down_lora_B"]
_OUT = ((8, 128, 256), "float32")


def kernel(**inputs):
    import numpy as _np
    import concourse.bacc as _bacc
    from concourse import mybir as _mybir
    from concourse.bass_utils import run_bass_kernel_spmd as _run

    nc = _bacc.Bacc("TRN2", target_bir_lowering=False, num_devices=1)
    arrays, args = {}, []
    for name in _INS:
        a = _np.ascontiguousarray(inputs[name])
        arrays[f"in_{name}"] = a
        args.append(nc.dram_tensor(f"in_{name}", a.shape, _mybir.dt.from_np(a.dtype), kind="ExternalInput").ap())
    args.append(nc.dram_tensor("out_0", _OUT[0], _mybir.dt.from_np(_np.dtype(_OUT[1])), kind="ExternalOutput").ap())
    cross_attention_moe_kernel(nc, *args)
    r = _run(nc, [arrays], core_ids=[0])
    return r.results[0]["out_0"]
```

```python
import concourse.bass as bass
from concourse import mybir
from contextlib import ExitStack

F32 = mybir.dt.float32
F32R = mybir.dt.float32r
BF16 = mybir.dt.bfloat16
ALU = mybir.AluOpType
ACT = mybir.ActivationFunctionType
AX = mybir.AxisListType


def cross_attention_moe_kernel(nc, x, ctx_kv, Wq, Wkv, Wout, gate_w, gate_A, gate_B,
                               gate_up, down, gup_A, gup_B, down_A, down_B, out):
    P = 128
    B, S, H = x.shape
    L = ctx_kv.shape[2]
    HD = 16
    NH = H // HD
    E = gate_w.shape[0]
    R = gate_A.shape[0]
    I = down.shape[1]
    HC = H // P
    NT = B
    GT = 4
    NG = NT // GT
    GN = GT * P
    NC = NH // 4
    VW = HD + 1
    SLOTS = ((0, 0, 3), (1, 3, 2), (2, 5, 1))
    KS = 6 * HD
    KM = KS + 3
    SCALE = 0.25
    LORA = 2.0
    EPS = 1e-5
    MASKED = -2.0 ** 127
    ONE_ONE = 1.00193786621093750
    ORDER = (2, 3, 0, 1)
    ROUTER_AT = GT + 1
    HEAD_AT = lambda i: i % HC * (NH // HC) + i // HC
    NM = (HC + 1) * E // 2
    EARLY = 6
    MERGE_BANK = lambda n: (3, 3, 4, 5, 6, 4)[n] if n < EARLY else 4
    MERGE_STEPS = NM - EARLY

    ctx = ExitStack()
    with ctx:
        def sb(name, shape, dt=F32):
            return ctx.enter_context(nc.sbuf_tensor(name, shape, dt))

        def sem(name):
            return ctx.enter_context(nc.semaphore(name))

        x_sb = sb("x_sb", [P, NT, H])
        ctx_sb = sb("ctx_sb", [P, NT, L])
        raw = sb("raw", [P, HC * H + 4 * HC * L])
        wq_raw = raw[:, 0:HC * H].rearrange("p (c n) -> p c n", c=HC)
        wkv_raw = raw[:, HC * H:HC * H + 2 * HC * L].rearrange("p (c l) -> p c l", c=2 * HC)
        wo_raw = sb("wo_raw", [P, HC, H])
        gw_raw = sb("gw_raw", [E, H])
        ga_raw = sb("ga_raw", [R, H])
        gb_raw = sb("gb_raw", [E, R])
        gbT = sb("gbT", [R, E])
        wqT_hi = sb("wqT_hi", [P, HC, H], F32R)
        wqT_lo = sb("wqT_lo", [P, HC, H], F32R)
        wkv_hi = sb("wkv_hi", [P, 2 * H], F32R)
        wkv_lo = sb("wkv_lo", [P, 2 * H], F32R)
        woT_hi = sb("woT_hi", [P, HC, H], F32R)
        woT_lo = sb("woT_lo", [P, HC, H], F32R)
        wr_hi = sb("wr_hi", [P, HC, P], F32R)
        wr_lo = sb("wr_lo", [P, HC, P], F32R)
        upA_raw = sb("upA_raw", [P, H])
        upB_raw = sb("upB_raw", [P, HC, E, R])
        dnA_raw = sb("dnA_raw", [P, I])
        dnB_raw = sb("dnB_raw", [P, HC, E, R])
        loraBT = sb("loraBT", [P, 2, H])
        expert_rows = sb("expert_rows", [P, E])
        up_w = sb("up_w", [P, HC, E, 2 * I])
        dn_w = sb("dn_w", [P, E, H])
        ffn_buf = up_w[:, :, :, :].rearrange("p a e n -> p (a e n)")
        silu = ffn_buf[:, 0:2 * GN].rearrange("p (k n) -> p k n", k=2)
        gated = ffn_buf[:, 2 * GN:4 * GN].rearrange("p (k n) -> p k n", k=2)
        h_f = ffn_buf[:, 4 * GN:6 * GN].rearrange("p (k n) -> p k n", k=2)
        up_hi = sb("up_hi", [P, HC, E, 2 * I], F32R)
        dn_hi = sb("dn_hi", [P, E, H], F32R)
        probsT = sb("probsT", [P, 2, NH, P])
        weight_all = probsT[:, :, :, :].rearrange("p k h n -> p (k h n)").rearrange("p (e n) -> p e n", e=E)
        q_st = sb("q_st", [KM, 3, NH, P], BF16)
        k_st = sb("k_st", [KM, 3, NH, P], BF16)
        v_sb = sb("v_sb", [P, NT, NH, VW])
        xT_hi = sb("xT_hi", [P, HC, NT * P], F32R)
        xT_lo = sb("xT_lo", [P, HC, NT * P], F32R)
        ident = sb("ident", [P, P])
        ident_b = sb("ident_b", [P, P], BF16)
        causal = sb("causal", [P, 4, P], BF16)
        stats = sb("stats", [P, 2, NT, 6])
        mv = sb("mv", [P, 2, NT, 2])
        rstd = sb("rstd", [P, 2, NT])
        var_eps = sb("var_eps", [P, NT])
        minus_half = sb("minus_half", [P, NT])
        m_sb = sb("m_sb", [P, 2, NH])
        m_rest = sb("m_rest", [P, NH])
        m_parts = sb("m_parts", [P, 3, NH], BF16)
        mT = sb("mT", [3 * NH, P], BF16)
        oT_sb = sb("oT_sb", [P, 4, P])
        r_den = sb("r_den", [P, NH])
        o_nat = sb("o_nat", [P, NH, HD])
        oT_hi = sb("oT_hi", [P, HC, P], F32R)
        oT_lo = sb("oT_lo", [P, HC, P], F32R)
        x2hat = sb("x2hat", [P, H])
        lgT = sb("lgT", [E, GN])
        lg = sb("lg", [P, GT, E])
        lmax = sb("lmax", [P, GT])
        above = sb("above", [P, GT, E, E])
        equal = sb("equal", [P, GT, E, E])
        earlier = sb("earlier", [P, E, E])
        rank = sb("rank", [P, GT, E])
        chosen = sb("chosen", [P, GT, E])
        lsub = sb("lsub", [P, GT, E])
        lexp = sb("lexp", [P, GT, E])
        lpick = sb("lpick", [P, GT, E])
        lsum = sb("lsum", [P, GT])
        linv = sb("linv", [P, GT])
        wts = sb("wts", [P, GT, E])
        wT = sb("wT", [E, NG, GN])
        dnA_bd = raw[:, :].rearrange("p (e n) -> p e n", e=E)
        with nc.sbuf_tensor("upA_bd", [P, E, H], F32) as upA_bd:
            pass
        h_hi = sb("h_hi", [P, 2, GN], F32R)
        h_lo = sb("h_lo", [P, 2, GN], F32R)

        with ExitStack() as early:
            def sbe(name, shape, dt=F32):
                return early.enter_context(nc.sbuf_tensor(name, shape, dt))
            parts = sbe("parts", [P, 2, 3, GT, HC, P], BF16)
            rest = sbe("rest", [P, 4, GN])
            xhat = sbe("xhat", [P, GT, H])
            cT = sbe("cT", [P, GN], F32R)
        up_lo = sb("up_lo", [P, HC, E, 2 * I], F32R)
        dn_lo = sb("dn_lo", [P, E, H], F32R)

        qk_dram = nc.dram_tensor("qk_parts", (2, NT, 3, HD, NH // HC, HC, P), BF16, kind="Internal").ap()

        w_dram = nc.dram_tensor("weights", (NG, E, GN), F32, kind="Internal").ap()

        bank = [ctx.enter_context(nc.psum_tensor(f"bank{i}", [P, 512], F32)) for i in range(8)]

        X2_BANK = lambda t: (bank[7][:, HC * P:2 * HC * P] if t < NT - 1 else bank[5][:, 0:HC * P])\
            .rearrange("p (a n) -> p a n", a=HC)
        QK_BANK = lambda j: bank[(5, 6, 7, 2)[j]]
        QK_PART = lambda j, t: parts[:, j // HC, t, :, j % HC, :]

        def merge_slice(w_up, w_dn, n):
            if n < HC * E // 2:
                c, e0 = divmod(2 * n, E)
                return w_up[:, c, e0:e0 + 2, :]
            e0 = 2 * n - HC * E
            return w_dn[:, e0:e0 + 2, :]

        ld = {n: sem("ld_" + n) for n in ("x0", "x1", "ctx", "wq", "wkv", "wo", "gate", "upA", "upB",
                                          "dnA", "dnB", "up", "dn")}
        stack_loaded = [sem(f"stack_loaded{i}") for i in range(3)]
        m_loaded = [sem(f"m_loaded{i}") for i in range(2)]
        weight_loaded = [sem(f"weight_loaded{e}") for e in range(E)]
        made = {}

        def S_(name):
            if name not in made:
                made[name] = sem(name)
            return made[name]

        xT_src = lambda g: slice(g * GN, (g + 1) * GN)
        ctx_v = ctx_kv.rearrange("b s l -> s b l")
        x_v = x.rearrange("b s h -> s b h")
        out_v = out.rearrange("b s h -> s b h")
        wkv_v = Wkv.rearrange("(c p) l -> p c l", p=P)

        block = ctx.enter_context(nc.Block())

        @block.sync
        def _(sp):
            sp.dma_start(x_sb[:, 0:GT, :], x_v[:, 0:GT, :]).then_inc(ld["x0"], 16)
            sp.dma_start(wkv_raw, wkv_v).then_inc(ld["wkv"], 16)
            sp.dma_start(ctx_sb[:, :, :], ctx_v).then_inc(ld["ctx"], 16)
            sp.dma_start(wq_raw, Wq.rearrange("(c p) h -> p c h", p=P)).then_inc(ld["wq"], 16)
            sp.dma_start(x_sb[:, GT:NT, :], x_v[:, GT:NT, :]).then_inc(ld["x1"], 16)
            sp.dma_start(upA_raw[:, :], gup_A.rearrange("e r h -> (e r) h")).then_inc(ld["upA"], 16)
            sp.dma_start(dnA_raw[:, :], down_A.rearrange("e r i -> (e r) i")).then_inc(ld["dnA"], 16)
            for c in range(HC):
                sp.dma_start(upB_raw[:, c, :, :], gup_B.rearrange("e (c p) r -> c p e r", p=P)[c]).then_inc(ld["upB"], 16)
            for c in range(HC):
                sp.dma_start(dnB_raw[:, c, :, :], down_B.rearrange("e (c p) r -> c p e r", p=P)[c]).then_inc(ld["dnB"], 16)
            sp.dma_start(wo_raw[:, :, :], Wout.rearrange("(c p) h -> p c h", p=P)).then_inc(ld["wo"], 16)
            sp.dma_start(gw_raw[:, :], gate_w).then_inc(ld["gate"], 16)
            sp.dma_start(ga_raw[:, :], gate_A).then_inc(ld["gate"], 16)
            sp.dma_start(gb_raw[:, :], gate_B).then_inc(ld["gate"], 16)
            for c in range(HC):
                sp.dma_start(up_w[:, c, :, :], gate_up.rearrange("e (c p) o -> c p e o", p=P)[c]).then_inc(ld["up"], 16)
            sp.dma_start(dn_w[:, :, :], down.rearrange("e i h -> i e h")).then_inc(ld["dn"], 16)

            def write_parts(g, which):
                sp.wait_ge(S_("k_part3" if which else "q_part3"), HC * (g + 1))
                for t in range(3):
                    dst = qk_dram[which, g * GT:(g + 1) * GT, t].rearrange("t d h c n -> (d h) t (c n)")
                    sp.dma_start(dst, parts[:, which, t, :, :, :].rearrange("p t c n -> p t (c n)"))\
                        .then_inc(S_("k_written" if which else "q_written"), 16)

            def load_stack(b):
                if b >= 3:
                    sp.wait_ge(S_("sT_ready"), NC * (b - 2))
                sp.wait_ge(S_("k_written"), 16 * 3 * (b // GT + 1))
                for _, first, count in SLOTS:
                    src = qk_dram[1, b, 0:count].rearrange("s d h c n -> (s d) (h c n)")
                    dst = k_st[first * HD:(first + count) * HD, b % 3, :, :].rearrange("p h n -> p (h n)")
                    sp.dma_start(dst, src).then_inc(stack_loaded[b % 3], 16)
                sp.wait_ge(S_("q_written"), 16 * 3 * (b // GT + 1))
                for part, first, count in SLOTS:
                    src = qk_dram[0, b, part].rearrange("d h c n -> d (h c n)")[None].to_broadcast([count, HD, NH * P])
                    dst = q_st[first * HD:(first + count) * HD, b % 3, :, :].rearrange("p h n -> p (h n)")
                    sp.dma_start(dst, src).then_inc(stack_loaded[b % 3], 16)

            def load_max(b):
                sp.wait_ge(S_("mT_copied"), b + 1)
                sp.dma_start(q_st[KS:KM, b % 3, :, :], mT[:, :]).then_inc(m_loaded[b % 2], 16)

            write_parts(0, 1)
            write_parts(0, 0)
            for b in range(3):
                load_stack(b)
            load_max(0)
            write_parts(1, 1)
            for b in range(NT):
                if b + 1 < NT:
                    load_max(b + 1)
                if b == 0:
                    write_parts(1, 0)
                if b + 3 < NT:
                    load_stack(b + 3)
            for g in range(NG):
                sp.wait_ge(S_("wT_copied"), g + 1)
                sp.dma_start(w_dram[g], wT[:, g, :]).then_inc(S_("w_written"), 16)
                sp.wait_ge(S_("w_written"), 16 * (g + 1))
                for e in range(E):
                    if g == 0:
                        sp.wait_ge(S_("pv_done"), NT - 1 if e < E // 2 else NT)
                    else:
                        sp.wait_ge(S_("h_ready"), e + 1)
                    sp.dma_start(weight_all[:, e, :], w_dram[g, e:e + 1, :].to_broadcast([P, GN])).then_inc(weight_loaded[e], 16)
            for g in range(NG):
                for k in range(2):
                    sp.wait_ge(S_("out_ready"), 2 * g + k + 1)
                    t0 = g * GT + 2 * k
                    sp.dma_start(out_v[:, t0:t0 + 2, :], x_sb[:, t0:t0 + 2, :]).then_inc(S_("stored"), 16)
            sp.wait_ge(S_("stored"), 16 * 2 * NG)

        @block.gpsimd
        def _(pool):
            step = [0]

            def link(ins):
                step[0] += 1
                ins.then_inc(S_("pool_chain"), 1)
                pool.wait_ge(S_("pool_chain"), step[0])

            link(pool.memset(minus_half[:, :], -0.5))
            link(pool.memset(ident[:, :], 0.0))
            link(pool.affine_select(out=ident[:, :], in_=ident[:, :], compare_op=ALU.not_equal, fill=1.0,
                                    base=0, pattern=[[-1, P]], channel_multiplier=1))
            pool.tensor_copy(ident_b[:, :], ident[:, :]).then_inc(S_("ident_made"), 1)

            def k_third_parts(g):
                for i in range(HC):
                    pool.wait_ge(S_("part2"), 4 * g + i + 1)
                    pool.tensor_tensor(QK_PART(ORDER[i], 2), rest[:, i, :].rearrange("p (t n) -> p t n", t=GT),
                                       QK_PART(ORDER[i], 1), ALU.subtract).then_inc(S_("k_part3"), 1)

            def normaliser(which, lo, hi, name, n):
                pool.wait_ge(S_(name), n)
                link(pool.tensor_scalar(var_eps[:, lo:hi], mv[:, which, lo:hi, 1], EPS, None, ALU.add))
                pool.tensor_tensor(rstd[:, which, lo:hi], var_eps[:, lo:hi], minus_half[:, lo:hi], ALU.pow)\
                    .then_inc(S_("rstd1_ready" if which == 0 else "rstd2_ready"), 1)

            pool.wait_ge(S_("ident_made"), 1)
            pool.memset(k_st[KS:KM, :, :, :].bitcast(F32), ONE_ONE).then_inc(S_("k_ones"), 1)
            pool.wait_ge(S_("k_ones"), 1)
            link(pool.memset(expert_rows[:, :], 1.0))
            link(pool.affine_select(out=expert_rows[:, :], in_=expert_rows[:, :], compare_op=ALU.is_ge, fill=0.0,
                                    base=0, pattern=[[-R, E]], channel_multiplier=1))
            link(pool.affine_select(out=expert_rows[:, :], in_=expert_rows[:, :], compare_op=ALU.is_ge, fill=0.0,
                                    base=R - 1, pattern=[[R, E]], channel_multiplier=-1))
            normaliser(0, 0, GT, "mv1_ready", GT)
            link(pool.memset(causal[:, :, :], 0.0))
            pool.affine_select(out=causal[:, :, :], in_=causal[:, :, :], compare_op=ALU.is_ge, fill=MASKED,
                               base=0, pattern=[[0, 4], [-1, P]], channel_multiplier=1).then_inc(S_("causal_made"), 1)

            pool.wait_ge(ld["upA"], 16)
            pool.tensor_tensor(upA_bd[:, :, :], upA_raw[:, None, :].to_broadcast([P, E, H]),
                               expert_rows[:, :, None].to_broadcast([P, E, H]), ALU.mult).then_inc(S_("upA_spread"), 1)
            normaliser(0, GT, NT, "mv1_ready", NT)
            pool.memset(v_sb[:, :, :, HD:VW], 1.0).then_inc(S_("v_ones"), 1)
            k_third_parts(0)
            pool.wait_ge(ld["dnA"], 16)
            pool.wait_ge(S_("wq_T"), 1)
            pool.wait_ge(S_("wkv_T"), 1)
            pool.tensor_tensor(dnA_bd, dnA_raw[:, None, :].to_broadcast([P, E, I]),
                               expert_rows[:, :, None].to_broadcast([P, E, I]), ALU.mult).then_inc(S_("dnA_spread"), 1)
            k_third_parts(1)
            link(pool.memset(earlier[:, :, :], 1.0))
            pool.affine_select(out=earlier[:, :, :], in_=earlier[:, :, :], compare_op=ALU.is_ge, fill=0.0,
                               base=-1, pattern=[[1, E], [-1, E]], channel_multiplier=0).then_inc(S_("router_consts"), 1)
            pool.wait_ge(S_("router_consts"), 1)

            def merge_low(n):
                if n == 0:
                    pool.wait_ge(S_("k_written"), 16 * 3 * NG)
                    pool.wait_ge(S_("q_written"), 16 * 3 * NG)
                    pool.wait_ge(S_("k_part3"), 2 * NG)
                    pool.wait_ge(S_("q_part3"), 2 * NG)
                    pool.wait_ge(S_("v_proj"), 2 * NG)
                    pool.wait_ge(S_("q_proj"), 2 * NG)
                pool.wait_ge(S_("highs_ready"), n + 1)
                pool.tensor_tensor(merge_slice(up_lo, dn_lo, n), merge_slice(up_w, dn_w, n),
                                   merge_slice(up_hi, dn_hi, n).bitcast(F32), ALU.subtract).then_inc(S_("lows_ready"), 1)

            def mask_chunk(b, c):
                pool.wait_ge(S_("exp_done"), NC * b + c + 1)
                ch = probsT[:, b % 2, 4 * c:4 * c + 4, :]
                pool.affine_select(out=ch, in_=ch, compare_op=ALU.is_ge, fill=0.0, base=0,
                                   pattern=[[0, 4], [1, P]], channel_multiplier=-1).then_inc(S_("probs_ready"), 1)

            mask_chunk(0, 0)
            mask_chunk(0, 1)
            for b in range(NT + 1):
                if b < NT:
                    mask_chunk(b, 2)
                    mask_chunk(b, 3)
                if 1 <= b <= NM // 2:
                    merge_low(2 * b - 2)
                    merge_low(2 * b - 1)
                if b >= 1:
                    normaliser(1, b - 1, b, "mv2_ready", b)
                if b + 1 < NT:
                    mask_chunk(b + 1, 0)
                    mask_chunk(b + 1, 1)

        @block.scalar
        def _(act):
            def high(out_, in_, done, scale=1.0):
                act.activation(out_, in_, ACT.Copy, scale=scale).then_inc(S_(done), 1)

            def first_part(g, i):
                j = ORDER[i]
                act.wait_ge(S_("q_proj" if j < HC else "k_proj"), HC * g + j % HC + 1)
                if g:
                    act.wait_ge(S_("q_written" if j < HC else "k_written"), 16 * 3 * g)
                high(QK_PART(j, 0), QK_BANK(j)[:, :].rearrange("p (t n) -> p t n", t=GT), "part1")

            def second_part(g, i):
                act.wait_ge(S_("rest_ready"), 4 * g + i + 1)
                high(QK_PART(ORDER[i], 1), rest[:, i, :].rearrange("p (t n) -> p t n", t=GT), "part2")

            act.wait_ge(S_("wkv_T"), 1)
            high(wkv_hi[:, 0:H].rearrange("p (a d h) -> p a h d", a=HC, d=HD),
                 bank[3][:, 0:H].rearrange("p (a h d) -> p a h d", a=HC, d=HD), "wkv_hi_ready")
            high(wkv_hi[:, H:2 * H], bank[3][:, H:2 * H], "wkv_hi_ready")
            act.wait_ge(S_("wq_T"), 1)
            for ic in range(HC):
                high(wqT_hi[:, ic, :].rearrange("p (a d h) -> p a h d", a=HC, d=HD),
                     bank[2][:, ic * H:(ic + 1) * H].rearrange("p (a h d) -> p a h d", a=HC, d=HD), "wq_hi_ready", SCALE)
            for g in range(NG):
                act.wait_ge(S_("c_T"), g + 1)
                if g:
                    act.wait_ge(S_("v_proj"), 2 * g)
                    act.wait_ge(S_("cT_lo"), g)
                high(cT[:, :], bank[4][:, :], "cT_hi")
                for ic in range(HC):
                    act.wait_ge(S_("x_T"), HC * g + ic + 1)
                    high(xT_hi[:, ic, xT_src(g)], bank[ic][:, :], "xT_hi_ready")
                first_part(g, 0)
                first_part(g, 1)
                for k in range(2):
                    act.wait_ge(S_("v_proj"), 2 * g + k + 1)
                    t0 = g * GT + 2 * k
                    high(v_sb[:, t0:t0 + 2, :, 0:HD],
                         bank[3 + k][:, :].rearrange("p (t h d) -> p t h d", t=2, d=HD), "v_ready")
                second_part(g, 0)
                second_part(g, 1)
                if g == 1:
                    act.wait_ge(S_("wo_T"), 1)
                    high(woT_hi[:, :, :].rearrange("p a n -> p (a n)"), bank[0][:, :], "wo_hi_ready")
                    act.wait_ge(S_("wr_T"), 1)
                    act.wait_ge(S_("wr_zero"), 2)
                    high(wr_hi[:, :, 0:E], bank[1][:, 0:HC * E].rearrange("p (a e) -> p a e", a=HC), "wr_hi_ready")
                first_part(g, 2)
                first_part(g, 3)
                second_part(g, 2)
                second_part(g, 3)
                if g == 0:
                    act.wait_ge(S_("gb_T"), 1)
                    high(gbT[:, :], bank[3][0:R, 0:E], "gbT_ready", LORA)
            def merge_high(n):
                act.wait_ge(S_("merged"), n + 1)
                high(merge_slice(up_hi, dn_hi, n), merge_slice(up_w, dn_w, n), "highs_ready")

            def copy_logits(g, bk):
                act.wait_ge(S_("lgT_ready"), g + 1)
                high(lgT[:, :], bk[0:E, :], "lgT_copied")

            def exp_logits(g):
                act.wait_ge(S_("lsub_ready"), g + 1)
                act.activation(lexp[:, :, :], lsub[:, :, :], ACT.Exp).then_inc(S_("lexp_ready"), 1)

            def copy_weights(g, bk):
                act.wait_ge(S_("wT_ready"), g + 1)
                act.activation(wT[:, g, :], bk[0:E, :], ACT.Copy).then_inc(S_("wT_copied"), 1)

            def mT_copy(b):
                act.wait_ge(S_("mT_ready"), b + 1)
                if b:
                    act.wait_ge(m_loaded[(b - 1) % 2], 16 * ((b - 1) // 2 + 1))
                act.activation(mT[:, :], bank[6][0:3 * NH, HC * P:HC * P + P // 2].bitcast(BF16), ACT.Copy).then_inc(S_("mT_copied"), 1)

            def exp_chunk(b, c):
                act.wait_ge(S_("sT_ready"), NC * b + c + 1)
                if b >= 2 and c == 0:
                    act.wait_ge(S_("pv_done"), b - 1)
                act.activation(probsT[:, b % 2, 4 * c:4 * c + 4, :].rearrange("p h n -> p (h n)"),
                               bank[2 + c % 2][:, :], ACT.Exp).then_inc(S_("exp_done"), 1)

            def silu_step(n):
                act.wait_ge(S_("gate_ready"), n + 1)
                if n >= 2:
                    act.wait_ge(S_("gated_ready"), n - 1)
                act.activation(silu[:, n % 2, :], bank[n % 2][:, :], ACT.Silu).then_inc(S_("silu_ready"), 1)

            def x2T_high(t):
                act.wait_ge(S_("x2_T"), t + 1)
                high(xT_hi[:, :, t * P:(t + 1) * P], X2_BANK(t), "x2T_hi")

            merge_high(0)
            mT_copy(0)
            merge_high(1)
            merge_high(2)
            exp_chunk(0, 0)
            exp_chunk(0, 1)
            merge_high(3)
            merge_high(4)
            for b in range(NT + 1):
                if b >= 1:
                    act.wait_ge(S_("pv_done"), b)
                    if b >= 2:
                        act.wait_ge(S_("on_ready"), b - 1)
                    high(oT_sb[:, :, :].rearrange("p a n -> p (a n)"), bank[4][:, :], "oT_copied")
                if b < NT:
                    exp_chunk(b, 2)
                if b + 1 < NT:
                    mT_copy(b + 1)
                if b < NT:
                    exp_chunk(b, 3)
                if b >= 2:
                    x2T_high(b - 2)
                if b == ROUTER_AT + 1:
                    exp_logits(0)
                if b >= 1:
                    act.wait_ge(S_("o_T"), b)
                    if b >= 2:
                        act.wait_ge(S_("o_out"), b - 1)
                    high(oT_hi[:, :, :].rearrange("p a n -> p (a n)"), bank[6][:, 0:HC * P], "oT_hi_ready")
                if b == 0:
                    merge_high(5)
                if b < MERGE_STEPS:
                    merge_high(EARLY + b)
                if b == ROUTER_AT + 2:
                    copy_weights(0, bank[5])
                if b + 1 < NT:
                    exp_chunk(b + 1, 0)
                    exp_chunk(b + 1, 1)
                if b == ROUTER_AT:
                    copy_logits(0, bank[6])
                if b == NT - 1:
                    act.wait_ge(S_("lows_ready"), NM)
                    silu_step(0)
            silu_step(1)

            def h_high(n):
                k = n % 2
                act.wait_ge(S_("h_ready"), n + 1)
                if n >= 2:
                    act.wait_ge(S_("down_done"), n - 1)
                high(h_hi[:, k, :], h_f[:, k, :], "h_hi_ready")

            h_high(0)
            silu_step(2)
            for n in range(NG * E):
                if n + 1 < NG * E:
                    h_high(n + 1)
                if 0 < n < NG * E - 2:
                    silu_step(n + 2)
                if n == 1:
                    x2T_high(NT - 1)
                if n == 2:
                    copy_logits(1, bank[5])
                if n == 4:
                    exp_logits(1)
                if n == 5:
                    copy_weights(1, bank[5])

        @block.vector
        def _(dve):
            step = [0]

            def link(ins):
                step[0] += 1
                ins.then_inc(S_("dve_chain"), 1)
                dve.wait_ge(S_("dve_chain"), step[0])

            def low(out_, in_, hi, done, scale=1.0):
                dve.scalar_tensor_tensor(out=out_, in0=in_, scalar=scale, in1=hi.bitcast(F32), op0=ALU.mult,
                                         op1=ALU.subtract).then_inc(S_(done), 1)

            def norm_stats(which, t, done):
                link(dve.bn_stats(stats[:, which, t, :], x_sb[:, t, :]))
                dve.bn_aggr(mv[:, which, t, :], stats[:, which, t, :]).then_inc(S_(done), 1)

            def normalise(which, t, out_, done):
                dve.tensor_scalar(out_, x_sb[:, t, :], mv[:, which, t, 0:1], rstd[:, which, t:t + 1],
                                  ALU.subtract, ALU.mult).then_inc(S_(done), 1)

            def normalise_group(g):
                dve.wait_ge(S_("rstd1_ready"), g + 1)
                if g:
                    dve.wait_ge(S_("x_T"), HC * g)
                for t in range(GT):
                    normalise(0, g * GT + t, xhat[:, t, :], "xhat_ready")

            dve.memset(wkv_lo[L:P, :].bitcast(F32), 0.0).then_inc(S_("wkv_zero"), 1)
            dve.memset(wr_hi[:, :, :].bitcast(F32), 0.0).then_inc(S_("wr_zero"), 1)
            dve.memset(wr_lo[:, :, :].bitcast(F32), 0.0).then_inc(S_("wr_zero"), 1)
            def group_stats(g):
                dve.wait_ge(ld[f"x{g}"], 16)
                for t in range(g * GT, (g + 1) * GT):
                    norm_stats(0, t, "mv1_ready")

            def input_lows(g):
                dve.wait_ge(S_("cT_hi"), g + 1)
                low(cT[L:P, :], bank[4][L:P, :], cT[L:P, :], "cT_lo")
                for ic in range(HC):
                    dve.wait_ge(S_("xT_hi_ready"), HC * g + ic + 1)
                    low(xT_lo[:, ic, xT_src(g)], bank[ic][:, :], xT_hi[:, ic, xT_src(g)], "xT_lo_ready")

            def remainder(g, i):
                j = ORDER[i]
                dve.wait_ge(S_("part1"), 4 * g + i + 1)
                if g:
                    if i < HC:
                        dve.wait_ge(S_("k_part3"), HC * (g - 1) + i + 1)
                    else:
                        dve.wait_ge(S_("q_part3"), HC * (g - 1) + i - HC + 1)
                dve.tensor_tensor(rest[:, i, :].rearrange("p (t n) -> p t n", t=GT),
                                  QK_BANK(j)[:, :].rearrange("p (t n) -> p t n", t=GT), QK_PART(j, 0), ALU.subtract)\
                    .then_inc(S_("rest_ready"), 1)

            def q_third_part(g, i):
                dve.wait_ge(S_("part2"), 4 * g + i + 1)
                dve.tensor_tensor(QK_PART(ORDER[i], 2), rest[:, i, :].rearrange("p (t n) -> p t n", t=GT),
                                  QK_PART(ORDER[i], 1), ALU.subtract).then_inc(S_("q_part3"), 1)

            def merge(n):
                if n == 0:
                    dve.wait_ge(ld["up"], 32)
                if n == HC * E // 2:
                    dve.wait_ge(ld["dn"], 16)
                dve.wait_ge(S_("lora_product"), n + 1)
                w = merge_slice(up_w, dn_w, n)
                dve.tensor_tensor(w, bank[MERGE_BANK(n)][:, :].rearrange("p (e n) -> p e n", e=2), w, ALU.add)\
                    .then_inc(S_("merged"), 1)

            group_stats(0)
            dve.wait_ge(S_("wkv_hi_ready"), 2)
            for a in range(HC):
                cols = slice(a * P, (a + 1) * P)
                low(wkv_lo[0:L, cols].rearrange("p (d h) -> p h d", d=HD),
                    bank[3][0:L, cols].rearrange("p (h d) -> p h d", d=HD),
                    wkv_hi[0:L, cols].rearrange("p (d h) -> p h d", d=HD), "wkv_lo_ready")
            low(wkv_lo[0:L, H:2 * H], bank[3][0:L, H:2 * H], wkv_hi[0:L, H:2 * H], "wkv_lo_ready")
            normalise_group(0)
            dve.wait_ge(S_("wq_hi_ready"), 2)
            for ic in range(HC):
                for a in range(HC):
                    cols = slice(a * P, (a + 1) * P)
                    low(wqT_lo[:, ic, cols].rearrange("p (d h) -> p h d", d=HD),
                        bank[2][:, ic * H + a * P:ic * H + (a + 1) * P].rearrange("p (h d) -> p h d", d=HD),
                        wqT_hi[:, ic, cols].rearrange("p (d h) -> p h d", d=HD), "wq_lo_ready", SCALE)
            input_lows(0)
            group_stats(1)
            remainder(0, 0)
            remainder(0, 1)
            normalise_group(1)
            remainder(0, 2)
            remainder(0, 3)
            q_third_part(0, 2)
            q_third_part(0, 3)
            dve.wait_ge(S_("lora_T"), 1)
            dve.tensor_scalar(loraBT[:, :, :].rearrange("p a n -> p (a n)"), bank[3][:, :], LORA, None, ALU.mult)\
                .then_inc(S_("lora_ready"), 1)
            input_lows(1)
            merge(0)
            remainder(1, 0)
            remainder(1, 1)
            dve.wait_ge(S_("wo_hi_ready"), 1)
            low(woT_lo[:, :, :].rearrange("p a n -> p (a n)"), bank[0][:, :],
                woT_hi[:, :, :].rearrange("p a n -> p (a n)"), "wo_lo_ready")
            dve.wait_ge(S_("wr_hi_ready"), 1)
            low(wr_lo[:, :, 0:E], bank[1][:, 0:HC * E].rearrange("p (a e) -> p a e", a=HC), wr_hi[:, :, 0:E], "wr_lo_ready")

            remainder(1, 2)
            remainder(1, 3)

            def max_chunk(b, c):
                dve.wait_ge(S_("s_ready"), NC * b + c + 1)
                dve.reduce_max(m_sb[:, b % 2, 4 * c:4 * c + 4], bank[c % 2][:, :].rearrange("p (h n) -> p h n", h=4), AX.X)\
                    .then_inc(S_("max_done"), 1)

            def h_low(n):
                k = n % 2
                dve.wait_ge(S_("h_hi_ready"), n + 1)
                dve.tensor_tensor(h_lo[:, k, :], h_f[:, k, :], h_hi[:, k, :].bitcast(F32), ALU.subtract)\
                    .then_inc(S_("h_lo_ready"), 1)

            def max_parts(b):
                m = m_sb[:, b % 2, :]
                dve.wait_ge(S_("max_done"), NC * (b + 1))
                if b:
                    dve.wait_ge(S_("mT_ready"), b)
                link(dve.tensor_scalar(m_parts[:, 0, :], m, -1.0, None, ALU.mult))
                link(dve.scalar_tensor_tensor(out=m_rest[:, :], in0=m, scalar=-1.0, in1=m_parts[:, 0, :],
                                              op0=ALU.mult, op1=ALU.subtract))
                link(dve.tensor_copy(m_parts[:, 1, :], m_rest[:, :]))
                dve.tensor_tensor(m_parts[:, 2, :], m_rest[:, :], m_parts[:, 1, :], ALU.subtract)\
                    .then_inc(S_("m_parts_ready"), 1)

            def route_logits(g, bk):
                dve.wait_ge(S_("lg_ready"), g + 1)
                link(dve.tensor_copy(lg[:, :, :], bk[:, 0:GT * E].rearrange("p (t e) -> p t e", e=E)))
                link(dve.reduce_max(lmax[:, :], lg[:, :, :], AX.X))
                dve.tensor_tensor(lsub[:, :, :], lg[:, :, :], lmax[:, :, None].to_broadcast([P, GT, E]), ALU.subtract)\
                    .then_inc(S_("lsub_ready"), 1)

            def route_choose(g):
                other = lg[:, :, None, :].to_broadcast([P, GT, E, E])
                mine = lg[:, :, :, None].to_broadcast([P, GT, E, E])
                link(dve.tensor_tensor(above[:, :, :, :], other, mine, ALU.is_gt))
                link(dve.tensor_tensor(equal[:, :, :, :], other, mine, ALU.is_equal))
                link(dve.tensor_tensor(equal[:, :, :, :], equal[:, :, :, :],
                                       earlier[:, None, :, :].to_broadcast([P, GT, E, E]), ALU.mult))
                link(dve.tensor_tensor(above[:, :, :, :], above[:, :, :, :], equal[:, :, :, :], ALU.add))
                link(dve.reduce_sum(rank[:, :, :], above[:, :, :, :], AX.X))
                link(dve.tensor_scalar(chosen[:, :, :], rank[:, :, :], 1.5, None, ALU.is_lt))

            def route_weights(g):
                dve.wait_ge(S_("lexp_ready"), g + 1)
                link(dve.tensor_tensor(lpick[:, :, :], lexp[:, :, :], chosen[:, :, :], ALU.mult))
                link(dve.reduce_sum(lsum[:, :], lpick[:, :, :], AX.X))
                link(dve.reciprocal(linv[:, :], lsum[:, :]))
                dve.tensor_tensor(wts[:, :, :], lpick[:, :, :], linv[:, :, None].to_broadcast([P, GT, E]), ALU.mult)\
                    .then_inc(S_("weights_ready"), 1)

            def add_residual(g):
                for k in range(2):
                    dve.wait_ge(S_("half_summed" if k == 0 else "down_done"), g + 1 if k == 0 else (g + 1) * E)
                    t0 = g * GT + 2 * k
                    dve.tensor_tensor(x_sb[:, t0:t0 + 2, :], bank[6 + k][:, :].rearrange("p (t n) -> p t n", t=2),
                                      x_sb[:, t0:t0 + 2, :], ALU.add).then_inc(S_("out_ready"), 1)

            def gate(n):
                k = n % 2
                if n == 0:
                    dve.wait_ge(S_("lows_ready"), NM)
                dve.wait_ge(S_("silu_ready"), n + 1)
                dve.wait_ge(S_("up_ready"), n + 1)
                dve.tensor_tensor(gated[:, k, :], bank[2 + k][:, :], silu[:, k, :], ALU.mult).then_inc(S_("gated_ready"), 1)

            def weigh(n):
                k = n % 2
                dve.wait_ge(S_("gated_ready"), n + 1)
                dve.wait_ge(weight_loaded[n % E], 16 * (n // E + 1))
                dve.tensor_tensor(h_f[:, k, :], weight_all[:, n % E, :], gated[:, k, :], ALU.mult).then_inc(S_("h_ready"), 1)

            for c in range(NC):
                max_chunk(0, c)
            max_parts(0)
            max_chunk(1, 0)
            merge(1)
            max_chunk(1, 1)
            merge(2)
            max_chunk(1, 2)
            merge(3)
            max_chunk(1, 3)
            merge(4)
            dve.wait_ge(S_("router_consts"), 1)
            def x2_normalise(t):
                dve.wait_ge(S_("rstd2_ready"), t + 1)
                if t:
                    dve.wait_ge(S_("x2_T"), t)
                normalise(1, t, x2hat[:, :], "x2hat_ready")

            def x2T_low(t):
                dve.wait_ge(S_("x2T_hi"), t + 1)
                low(xT_lo[:, :, t * P:(t + 1) * P], X2_BANK(t), xT_hi[:, :, t * P:(t + 1) * P], "x2T_lo")

            on = bank[5][:, :].rearrange("p (h w) -> p h w", h=NH)

            def softmax_denominators(b):
                dve.wait_ge(S_("on_ready"), b + 1)
                dve.reciprocal(r_den[:, :], on[:, :, HD]).then_inc(S_("r_den_ready"), 1)

            def softmax_divide(b):
                dve.wait_ge(S_("r_den_ready"), b + 1)
                dve.tensor_tensor(o_nat[:, :, :], on[:, :, 0:HD], r_den[:, :, None].to_broadcast([P, NH, HD]), ALU.mult)\
                    .then_inc(S_("o_nat_ready"), 1)

            for b in range(NT + 1):
                if b + 1 < NT:
                    max_parts(b + 1)
                if b == 0:
                    merge(5)
                    q_third_part(1, 2)
                    q_third_part(1, 3)
                if b >= 2:
                    x2_normalise(b - 2)
                if b >= 1:
                    softmax_denominators(b - 1)
                    softmax_divide(b - 1)
                if b == NT:
                    gate(0)
                if b == ROUTER_AT + 1:
                    route_logits(0, bank[1])
                if b < MERGE_STEPS:
                    merge(EARLY + b)
                if b >= 2:
                    x2T_low(b - 2)
                if b + 2 < NT:
                    max_chunk(b + 2, 0)
                if 1 <= b <= NT:
                    dve.wait_ge(S_("oT_hi_ready"), b)
                    low(oT_lo[:, :, :].rearrange("p a n -> p (a n)"), bank[6][:, 0:HC * P],
                        oT_hi[:, :, :].rearrange("p a n -> p (a n)"), "oT_lo_ready")
                if b + 2 < NT:
                    max_chunk(b + 2, 1)
                    max_chunk(b + 2, 2)
                if 1 <= b <= NT:
                    t = b - 1
                    if b == ROUTER_AT + 1:
                        route_choose(0)
                    if b == NT:
                        weigh(0)
                    dve.wait_ge(S_("o_out"), b)
                    dve.tensor_tensor(x_sb[:, t, :], bank[7][:, 0:H], x_sb[:, t, :], ALU.add).then_inc(S_("x1_ready"), 1)
                    if b == NT:
                        h_low(0)
                    dve.wait_ge(S_("x1_ready"), b)
                    norm_stats(1, t, "mv2_ready")
                if b + 2 < NT:
                    max_chunk(b + 2, 3)
                if b == ROUTER_AT + 1:
                    route_weights(0)

            gate(1)
            weigh(1)
            x2_normalise(NT - 1)
            gate(2)
            for n in range(NG * E):
                if n == E:
                    add_residual(0)
                if n == 1:
                    weigh(2)
                if n + 1 < NG * E:
                    h_low(n + 1)
                if 0 < n < NG * E - 2:
                    gate(n + 2)
                    weigh(n + 2)
                if n == 1:
                    x2T_low(NT - 1)
                if n == 3:
                    route_logits(1, bank[5])
                    route_choose(1)
                if n == 4:
                    route_weights(1)
            add_residual(1)

        @block.tensor
        def _(pe):
            def products(out_, pairs, done=None, start=True, stop=True, **kw):
                for i, (a, m) in enumerate(pairs):
                    last = pe.matmul(out_, a, m, start=start and i == 0, stop=stop and i == len(pairs) - 1, **kw)
                if done:
                    last.then_inc(S_(done), 1)

            def transpose_twice(out_, in_):
                pe.transpose(out_[0:L, :], in_, ident[:, :])
                return pe.matmul(out_[L:P, :], in_, ident[:, :], start=True, stop=True)

            pe.wait_ge(S_("ident_made"), 1)
            pe.wait_ge(ld["wkv"], 16)
            for oc in range(2 * HC):
                last = transpose_twice(bank[3][:, oc * P:(oc + 1) * P], wkv_raw[:, oc, :])
            last.then_inc(S_("wkv_T"), 1)

            def context_T(g):
                if g == 0:
                    pe.wait_ge(ld["ctx"], 16)
                else:
                    pe.wait_ge(S_("v_ready"), 2 * g)
                for t in range(GT):
                    last = transpose_twice(bank[4][:, t * P:(t + 1) * P], ctx_sb[:, g * GT + t, :])
                last.then_inc(S_("c_T"), 1)

            def x_T(g):
                pe.wait_ge(S_("xhat_ready"), GT * (g + 1))
                if g:
                    pe.wait_ge(S_("xT_lo_ready"), HC * g)
                for ic in range(HC):
                    for t in range(GT):
                        last = pe.transpose(bank[ic][:, t * P:(t + 1) * P], xhat[:, t, ic * P:(ic + 1) * P], ident[:, :])
                    last.then_inc(S_("x_T"), 1)

            def kv_proj(g):
                pe.wait_ge(S_("wkv_lo_ready"), HC + 1)
                pe.wait_ge(S_("wkv_zero"), 1)
                pe.wait_ge(S_("wkv_hi_ready"), 2)
                pe.wait_ge(S_("wq_lo_ready"), HC * HC)
                pe.wait_ge(S_("cT_lo"), g + 1)
                if g:
                    pe.wait_ge(S_("rest_ready"), 4 * g)
                    pe.wait_ge(S_("v_ready"), 2 * g)
                for oc in range(HC):
                    cols = slice(oc * P, (oc + 1) * P)
                    products(QK_BANK(HC + oc)[:, :], [(wkv_hi[:, cols], cT[:, :]), (wkv_lo[:, cols], cT[:, :])], "k_proj")
                if g:
                    pe.wait_ge(S_("merged"), 1)
                for k in range(2):
                    for t in range(2):
                        tok = slice((2 * k + t) * P, (2 * k + t + 1) * P)
                        products(bank[3 + k][:, t * H:(t + 1) * H],
                                 [(cT[:, tok], wkv_hi[:, H:2 * H]), (cT[:, tok], wkv_lo[:, H:2 * H])],
                                 "v_proj" if t else None)

            def q_proj(g):
                pe.wait_ge(S_("xT_lo_ready"), HC * (g + 1))
                for oc in range(HC):
                    cols = slice(oc * P, (oc + 1) * P)
                    products(QK_BANK(oc)[:, :],
                             [(w[:, ic, cols], xt[:, ic, xT_src(g)]) for ic in range(HC)
                              for w, xt in ((wqT_hi, xT_hi), (wqT_hi, xT_lo), (wqT_lo, xT_hi))], "q_proj")

            pe.wait_ge(ld["wq"], 16)
            for ic in range(HC):
                for oc in range(HC):
                    last = pe.transpose(bank[2][:, ic * H + oc * P:ic * H + (oc + 1) * P],
                                        wq_raw[:, oc, ic * P:(ic + 1) * P], ident[:, :])
            last.then_inc(S_("wq_T"), 1)
            context_T(0)
            x_T(0)
            kv_proj(0)
            q_proj(0)
            x_T(1)
            context_T(1)
            pe.wait_ge(ld["gate"], 48)
            pe.wait_ge(S_("v_ready"), 2)
            pe.transpose(bank[3][0:R, 0:E], gb_raw[:, :], ident[0:E, 0:E]).then_inc(S_("gb_T"), 1)
            pe.wait_ge(S_("gbT_ready"), 1)
            pe.wait_ge(ld["upB"], 32)
            pe.wait_ge(ld["dnB"], 32)
            for k, b_raw in enumerate((upB_raw, dnB_raw)):
                for c in range(HC):
                    last = pe.transpose(bank[3][:, k * H + c * P:k * H + (c + 1) * P],
                                        b_raw[:, c, :, :].rearrange("p e r -> p (e r)"), ident[:, :])
            last.then_inc(S_("lora_T"), 1)

            def lora_product(n):
                if n == 0:
                    pe.wait_ge(S_("lora_ready"), 1)
                    pe.wait_ge(S_("upA_spread"), 1)
                if n == 1:
                    pe.wait_ge(S_("v_ready"), 2 * NG)
                if n in (5, 6):
                    pe.wait_ge(S_("merged"), {5: 3, 6: 6}[n])
                if n == 3:
                    pe.wait_ge(S_("rest_ready"), 4 * NG)
                if n == 4:
                    pe.wait_ge(S_("mT_copied"), 1)
                if n == HC * E // 2:
                    pe.wait_ge(S_("dnA_spread"), 1)
                for k in range(2):
                    out_ = bank[MERGE_BANK(n)][:, k * H:(k + 1) * H]
                    if n < HC * E // 2:
                        c, e0 = divmod(2 * n, E)
                        pair = (upA_bd[:, e0 + k, c * P:(c + 1) * P], loraBT[:, 0, :])
                    else:
                        pair = (dnA_bd[:, 2 * n - HC * E + k, :], loraBT[:, 1, :])
                    products(out_, [pair], "lora_product" if k else None)

            lora_product(0)
            kv_proj(1)

            pe.wait_ge(ld["wo"], 16)
            pe.wait_ge(S_("xT_lo_ready"), HC * NG)
            for ic in range(HC):
                for oc in range(HC):
                    last = pe.transpose(bank[0][:, ic * H + oc * P:ic * H + (oc + 1) * P],
                                        wo_raw[:, oc, ic * P:(ic + 1) * P], ident[:, :])
            last.then_inc(S_("wo_T"), 1)
            for ic in range(HC):
                products(bank[1][:, ic * E:(ic + 1) * E],
                         [(gw_raw[:, ic * P:(ic + 1) * P], ident[0:E, 0:E]), (ga_raw[:, ic * P:(ic + 1) * P], gbT[:, :])],
                         "wr_T" if ic else None)
            q_proj(1)

            def s_chunk(b, c):
                n = NC * b + c
                if c == 0:
                    pe.wait_ge(stack_loaded[b % 3], 16 * 6 * (b // 3 + 1))
                if b == 0 and c == 0:
                    pe.wait_ge(S_("wo_lo_ready"), 1)
                    pe.wait_ge(S_("wr_lo_ready"), 1)
                if n >= 2:
                    pe.wait_ge(S_("max_done"), n - 1)
                pe.matmul(bank[c % 2][:, :], ident_b[:, :], causal[:, :, :].rearrange("p h n -> p (h n)"),
                          start=True, stop=True, skip_group_check=True)
                for j in range(4):
                    h = 4 * c + j
                    last = pe.matmul(bank[c % 2][:, j * P:(j + 1) * P], q_st[0:KS, b % 3, h, :], k_st[0:KS, b % 3, h, :],
                                     start=False, stop=True, skip_group_check=True)
                last.then_inc(S_("s_ready"), 1)

            def sT_chunk(b, c):
                n = NC * b + c
                if c == 0:
                    pe.wait_ge(m_loaded[b % 2], 16 * (b // 2 + 1))
                if n == 1:
                    pe.wait_ge(S_("merged"), 2)
                if n >= 2:
                    pe.wait_ge(S_("exp_done"), n - 1)
                for j in range(4):
                    h = 4 * c + j
                    last = pe.matmul(bank[2 + c % 2][:, j * P:(j + 1) * P], k_st[0:KM, b % 3, h, :], q_st[0:KM, b % 3, h, :],
                                     start=True, stop=True)
                last.then_inc(S_("sT_ready"), 1)

            def max_T(b):
                if b == 0:
                    pe.wait_ge(S_("rest_ready"), 4 * NG)
                if b > 2:
                    pe.wait_ge(S_("oT_lo_ready"), b - 2)
                if b == 1:
                    pe.wait_ge(S_("merged"), 5)
                if b == ROUTER_AT + 2:
                    pe.wait_ge(S_("lgT_copied"), 1)
                pe.wait_ge(S_("m_parts_ready"), b + 1)
                pe.transpose(bank[6][0:3 * NH, HC * P:HC * P + P // 2].bitcast(BF16), m_parts[:, :, :].rearrange("p t h -> p (t h)"),
                             ident_b[:, :]).then_inc(S_("mT_ready"), 1)

            def router_logits(g, bk):
                pe.wait_ge(S_("x2T_lo"), GT * (g + 1))
                products(bk[:, :], [(w[:, ic, :], xt[:, ic, xT_src(g)]) for ic in range(HC)
                                    for w, xt in ((wr_hi, xT_hi), (wr_hi, xT_lo), (wr_lo, xT_hi))], "lgT_ready")

            def lg_T(g, bk):
                pe.wait_ge(S_("lgT_copied"), g + 1)
                for t in range(GT):
                    last = pe.transpose(bk[:, t * E:(t + 1) * E], lgT[:, t * P:(t + 1) * P], ident[0:E, 0:E])
                last.then_inc(S_("lg_ready"), 1)

            def w_T(g, bk):
                pe.wait_ge(S_("weights_ready"), g + 1)
                for t in range(GT):
                    last = pe.transpose(bk[0:E, t * P:(t + 1) * P], wts[:, t, :], ident[:, :])
                last.then_inc(S_("wT_ready"), 1)

            def gate_up_half(n, half, done):
                g, e = divmod(n, E)
                cols = slice(half * I, (half + 1) * I)
                products(bank[2 * half + n % 2][:, :],
                         [(w[:, ic, e, cols], xt[:, ic, xT_src(g)]) for ic in range(HC)
                          for w, xt in ((up_hi, xT_hi), (up_hi, xT_lo), (up_lo, xT_hi))], done)

            def gate_step(n):
                if n >= 2:
                    pe.wait_ge(S_("silu_ready"), n - 1)
                gate_up_half(n, 0, "gate_ready")

            def up_step(n):
                if n >= 2:
                    pe.wait_ge(S_("gated_ready"), n - 1)
                gate_up_half(n, 1, "up_ready")

            def down_step(n):
                g, e = divmod(n, E)
                k = n % 2
                pe.wait_ge(S_("h_lo_ready"), n + 1)
                if n == 0:
                    pe.wait_ge(S_("x1_ready"), NT)
                    pe.wait_ge(S_("x2T_lo"), NT - 1)
                if e == 0 and g:
                    pe.wait_ge(S_("out_ready"), 2 * g)
                for t in range(GT):
                    tok = slice(t * P, (t + 1) * P)
                    for i, (a, w) in enumerate(((h_hi, dn_hi), (h_hi, dn_lo), (h_lo, dn_hi))):
                        last = pe.matmul(bank[6 + t // 2][:, (t % 2) * H:(t % 2 + 1) * H], a[:, k, tok], w[:, e, :],
                                         start=e == 0 and t % 2 == 0 and i == 0, stop=e == E - 1 and i == 2,
                                         skip_group_check=True)
                    if t == 1 and e == E - 1:
                        last.then_inc(S_("half_summed"), 1)
                last.then_inc(S_("down_done"), 1)

            pe.wait_ge(S_("causal_made"), 1)
            pe.wait_ge(S_("k_ones"), 1)
            pe.wait_ge(S_("v_ones"), 1)
            s_chunk(0, 0)
            s_chunk(0, 1)
            lora_product(1)
            s_chunk(0, 2)
            s_chunk(0, 3)
            lora_product(2)
            s_chunk(1, 0)
            max_T(0)
            s_chunk(1, 1)
            lora_product(3)
            s_chunk(1, 2)
            s_chunk(1, 3)
            lora_product(4)
            sT_chunk(0, 0)
            sT_chunk(0, 1)
            lora_product(5)

            def x2_T(t):
                pe.wait_ge(S_("x2hat_ready"), t + 1)
                for ic in range(HC):
                    last = pe.transpose(X2_BANK(t)[:, ic, :], x2hat[:, ic * P:(ic + 1) * P], ident[:, :])
                last.then_inc(S_("x2_T"), 1)

            for b in range(NT + 1):
                if b == NT:
                    up_step(1)
                if b < NT:
                    sT_chunk(b, 2)
                    sT_chunk(b, 3)
                if b == NT - 1:
                    pe.wait_ge(S_("lows_ready"), NM)
                    pe.wait_ge(S_("lsub_ready"), 1)
                    gate_step(1)
                if b + 1 < NT:
                    max_T(b + 1)
                if 1 <= b <= NT:
                    pe.wait_ge(S_("oT_copied"), b)
                    if b == 1:
                        pe.wait_ge(S_("merged"), 4)
                    if b == ROUTER_AT + 3:
                        pe.wait_ge(S_("wT_copied"), 1)
                    for c in range(4):
                        last = pe.transpose(bank[5][:, c * P:(c + 1) * P], oT_sb[:, c, :], ident[:, :])
                    last.then_inc(S_("on_ready"), 1)
                if b < MERGE_STEPS:
                    lora_product(EARLY + b)
                if b >= 2:
                    x2_T(b - 2)
                if b == ROUTER_AT + 1:
                    pe.wait_ge(S_("max_done"), NC * NT)
                    lg_T(0, bank[1])
                if b + 2 < NT:
                    s_chunk(b + 2, 0)
                if 1 <= b <= NT:
                    pe.wait_ge(S_("o_nat_ready"), b)
                    pe.wait_ge(S_("mT_copied"), min(b + 2, NT))
                    for ic in range(HC):
                        last = pe.transpose(bank[6][:, ic * P:(ic + 1) * P],
                                            o_nat[:, :, :].rearrange("p h d -> p (h d)")[:, ic * P:(ic + 1) * P], ident[:, :])
                    last.then_inc(S_("o_T"), 1)
                if b + 2 < NT:
                    s_chunk(b + 2, 1)
                    s_chunk(b + 2, 2)
                if b == NT - 2:
                    pe.wait_ge(S_("lows_ready"), E // 2 + 1)
                    pe.wait_ge(S_("max_done"), NC * NT)
                    gate_step(0)
                if b == ROUTER_AT + 2:
                    w_T(0, bank[5])
                if b == NT - 1:
                    pe.wait_ge(S_("exp_done"), NC * NT)
                    up_step(0)
                if b == NT:
                    gate_step(2)
                if 1 <= b <= NT:
                    pe.wait_ge(S_("oT_lo_ready"), b)
                    if b >= 2:
                        pe.wait_ge(S_("x2T_lo"), b - 1)
                    products(bank[7][:, 0:H], [(a[:, ic, :], w[:, ic, :]) for ic in range(HC)
                                               for a, w in ((oT_hi, woT_hi), (oT_hi, woT_lo), (oT_lo, woT_hi))], "o_out")
                if b == ROUTER_AT:
                    router_logits(0, bank[6])
                if b + 2 < NT:
                    s_chunk(b + 2, 3)
                if b + 1 < NT:
                    sT_chunk(b + 1, 0)
                    sT_chunk(b + 1, 1)
                if b < NT:
                    if b < MERGE_STEPS:
                        pe.wait_ge(S_("merged"), EARLY + b + 1)
                    for i in range(NH):
                        if i % 4 == 0:
                            pe.wait_ge(S_("probs_ready"), NC * b + i // 4 + 1)
                        if i == 0 and b:
                            pe.wait_ge(S_("oT_copied"), b)
                        h = HEAD_AT(i)
                        c, j = divmod(h, 4)
                        last = pe.matmul(bank[4][32 * j:32 * j + VW, c * P:(c + 1) * P], v_sb[:, b, h, :],
                                         probsT[:, b % 2, i, :], start=True, stop=True)
                    last.then_inc(S_("pv_done"), 1)

            for n in range(NG * E):
                if n == 0:
                    up_step(2)
                elif n + 2 < NG * E:
                    gate_step(n + 2)
                    up_step(n + 2)
                if n == 1:
                    x2_T(NT - 1)
                if n == 2:
                    router_logits(1, bank[5])
                if n == 3:
                    lg_T(1, bank[5])
                if n == 5:
                    w_T(1, bank[5])
                down_step(n)


_INS = ["x", "ctx_512", "L0_xattn_Wq", "L0_xattn_Wkv_expand", "L0_xattn_Wout", "L0_ffn_gate_weight",
        "L0_ffn_gate_lora_A", "L0_ffn_gate_lora_B", "L0_ffn_gate_up_proj", "L0_ffn_down_proj",
        "L0_ffn_gup_lora_A", "L0_ffn_gup_lora_B", "L0_ffn_down_lora_A", "L0_ffn_down_lora_B"]
_OUT = ((8, 128, 256), "float32")


def kernel(**inputs):
    import numpy as _np
    import concourse.bacc as _bacc
    from concourse import mybir as _mybir
    from concourse.bass_utils import run_bass_kernel_spmd as _run

    nc = _bacc.Bacc("TRN2", target_bir_lowering=False, num_devices=1)
    arrays, args = {}, []
    for name in _INS:
        a = _np.ascontiguousarray(inputs[name])
        arrays[f"in_{name}"] = a
        args.append(nc.dram_tensor(f"in_{name}", a.shape, _mybir.dt.from_np(a.dtype), kind="ExternalInput").ap())
    args.append(nc.dram_tensor("out_0", _OUT[0], _mybir.dt.from_np(_np.dtype(_OUT[1])), kind="ExternalOutput").ap())
    cross_attention_moe_kernel(nc, *args)
    r = _run(nc, [arrays], core_ids=[0])
    return r.results[0]["out_0"]
```
